# Optimizing a Trainium2 kernel written in Bass

```python
import numpy as np
import jax
import jax.numpy as jnp

def _softmax(x, axis=-1):
    return jax.nn.softmax(x, axis=axis)

def _gelu(x):
    return jax.nn.gelu(x, approximate=True)

def _silu(x):
    return jax.nn.silu(x)

def _sigmoid(x):
    return jax.nn.sigmoid(x)

def _layernorm(x, axis=-1, eps=1e-05):
    m = jnp.mean(x, axis=axis, keepdims=True)
    v = jnp.var(x, axis=axis, keepdims=True)
    return (x - m) / jnp.sqrt(v + eps)

def _scatter_add(tgt, idx, src, axis=0):
    return tgt.at[idx].add(src)

def _segment_sum(src, seg, n):
    return jax.ops.segment_sum(src, seg, n)
kernel_name = 'mk_seq_postln_d1_jaxref_r8_3b742f'

def setup_inputs(seed: int=0):
    np.random.seed(seed)
    _w = jnp.asarray

    def _L0_attn_setup():
        import jax, jax.numpy as jnp
        import numpy as np
        D_MODEL = 128
        N_HEADS = 16
        D_HEAD = D_MODEL // N_HEADS
        GN_EPS = 1e-05
        key = jax.random.key(seed)
        ks = jax.random.split(key, 5)
        B, T = (2, 256)
        s = 1.0 / np.sqrt(D_MODEL)
        x = jax.random.normal(ks[0], (B, T, D_MODEL), dtype=jnp.float32)
        W_q = jax.random.normal(ks[1], (D_MODEL, D_MODEL), dtype=jnp.float32) * s
        W_k = jax.random.normal(ks[2], (D_MODEL, D_MODEL), dtype=jnp.float32) * s
        W_v = jax.random.normal(ks[3], (D_MODEL, D_MODEL), dtype=jnp.float32) * s
        W_o = jax.random.normal(ks[4], (D_MODEL, D_MODEL), dtype=jnp.float32) * s
        gn_weight = jnp.ones((D_MODEL,), dtype=jnp.float32)
        gn_bias = jnp.zeros((D_MODEL,), dtype=jnp.float32)
        return {'x': x, 'W_q': W_q, 'W_k': W_k, 'W_v': W_v, 'W_o': W_o, 'gn_weight': gn_weight, 'gn_bias': gn_bias}
    _L0_attn_in = _L0_attn_setup()

    def _L0_ffn_setup():
        import jax, jax.numpy as jnp
        import numpy as np
        TOP_K = 2
        NUM_EXPERTS = 8
        DIM = 128
        HIDDEN = 352
        BS, SLEN = (2, 128)

        def _grouped_ffn(x, w1, w2, w3, counts):
            num_experts = w1.shape[0]
            ends = jnp.cumsum(counts)
            starts = ends - counts
            t = jnp.arange(x.shape[0])
            out = jnp.zeros((x.shape[0], w2.shape[-1]), x.dtype)
            for e in range(num_experts):
                m = ((t >= starts[e]) & (t < ends[e])).astype(x.dtype)[:, None]
                xe = x * m
                h = jax.nn.silu(xe @ w1[e]) * (xe @ w3[e])
                out = out + h @ w2[e] * m
            return out
        key = jax.random.key(seed)
        k = jax.random.split(key, 5)
        std = 0.02
        return {'x': jax.random.normal(k[0], (BS, SLEN, DIM), jnp.float32), 'gate_w': jax.random.normal(k[1], (NUM_EXPERTS, DIM), jnp.float32) * std, 'expert_bias': jnp.zeros((NUM_EXPERTS,), jnp.float32), 'w1': jax.random.normal(k[2], (NUM_EXPERTS, DIM, HIDDEN), jnp.float32) * std, 'w2': jax.random.normal(k[3], (NUM_EXPERTS, HIDDEN, DIM), jnp.float32) * std, 'w3': jax.random.normal(k[4], (NUM_EXPERTS, DIM, HIDDEN), jnp.float32) * std}
    _L0_ffn_in = _L0_ffn_setup()
    _d = {'L0_attn_x': _L0_attn_in['x'], 'L0_attn_W_q': _L0_attn_in['W_q'], 'L0_attn_W_k': _L0_attn_in['W_k'], 'L0_attn_W_v': _L0_attn_in['W_v'], 'L0_attn_W_o': _L0_attn_in['W_o'], 'L0_attn_gn_weight': _L0_attn_in['gn_weight'], 'L0_attn_gn_bias': _L0_attn_in['gn_bias'], 'L0_ffn_gate_w': _L0_ffn_in['gate_w'], 'L0_ffn_expert_bias': _L0_ffn_in['expert_bias'], 'L0_ffn_w1': _L0_ffn_in['w1'], 'L0_ffn_w2': _L0_ffn_in['w2'], 'L0_ffn_w3': _L0_ffn_in['w3']}
    _x0 = _d['L0_attn_x']
    _d['L0_attn_x'] = jax.random.normal(jax.random.fold_in(jax.random.key(seed), 1), (2, 1024, 128), dtype=_x0.dtype)
    del _x0
    return _d

def reference(L0_attn_x, L0_attn_W_q, L0_attn_W_k, L0_attn_W_v, L0_attn_W_o, L0_attn_gn_weight, L0_attn_gn_bias, L0_ffn_gate_w, L0_ffn_expert_bias, L0_ffn_w1, L0_ffn_w2, L0_ffn_w3):

    def _L0_attn_ref(x, W_q, W_k, W_v, W_o, gn_weight, gn_bias):
        import jax, jax.numpy as jnp
        import numpy as np
        D_MODEL = 128
        N_HEADS = 16
        D_HEAD = D_MODEL // N_HEADS
        GN_EPS = 1e-05
        B, T, _ = x.shape
        H, Dh = (N_HEADS, D_HEAD)
        q = (x @ W_q.T).reshape(B, T, H, Dh)
        k = (x @ W_k.T).reshape(B, T, H, Dh)
        v = (x @ W_v.T).reshape(B, T, H, Dh)
        gammas = jnp.asarray([1.0 - 2.0 ** (-5.0 - i) for i in range(H)], dtype=jnp.float32)
        idx = jnp.arange(T, dtype=jnp.float32)
        diff = idx[:, None] - idx[None, :]
        decay = jnp.where(diff >= 0, gammas[:, None, None] ** jnp.maximum(diff, 0.0), 0.0)
        scale = jnp.sqrt(jnp.asarray(Dh, dtype=x.dtype))
        qk = jnp.einsum('bthd,bshd->bhts', q, k)
        attn = qk * decay[None] / scale
        y = jnp.einsum('bhts,bshd->bthd', attn, v)
        yg = y.transpose(0, 2, 3, 1)
        mean = yg.mean(axis=(2, 3), keepdims=True)
        var = yg.var(axis=(2, 3), keepdims=True)
        yn = (yg - mean) / jnp.sqrt(var + GN_EPS)
        yn = yn * gn_weight.reshape(1, H, Dh, 1) + gn_bias.reshape(1, H, Dh, 1)
        y = yn.transpose(0, 3, 1, 2).reshape(B, T, H * Dh)
        return y @ W_o.T

    def _L0_ffn_ref(x, gate_w, expert_bias, w1, w2, w3):
        import jax, jax.numpy as jnp
        import numpy as np
        TOP_K = 2
        NUM_EXPERTS = 8
        DIM = 128
        HIDDEN = 352
        BS, SLEN = (2, 128)

        def _grouped_ffn(x, w1, w2, w3, counts):
            num_experts = w1.shape[0]
            ends = jnp.cumsum(counts)
            starts = ends - counts
            t = jnp.arange(x.shape[0])
            out = jnp.zeros((x.shape[0], w2.shape[-1]), x.dtype)
            for e in range(num_experts):
                m = ((t >= starts[e]) & (t < ends[e])).astype(x.dtype)[:, None]
                xe = x * m
                h = jax.nn.silu(xe @ w1[e]) * (xe @ w3[e])
                out = out + h @ w2[e] * m
            return out
        bs, slen, dim = x.shape
        num_experts = gate_w.shape[0]
        xf = x.reshape(bs * slen, dim)
        scores = jax.nn.softmax((xf @ gate_w.T).astype(jnp.float32), axis=-1)
        _, sel = jax.lax.top_k(scores + expert_bias, TOP_K)
        top_scores = jnp.take_along_axis(scores, sel, axis=1).reshape(-1)
        sel_flat = sel.reshape(-1)
        counts = jnp.zeros((num_experts,), jnp.int32).at[sel_flat].add(1)
        order = jnp.argsort(sel_flat, stable=True)
        top_scores_sorted = top_scores[order]
        token_idx = order // TOP_K
        routed = xf[token_idx] * top_scores_sorted[:, None].astype(xf.dtype)
        routed_out = _grouped_ffn(routed, w1, w2, w3, counts)
        out = jnp.zeros_like(xf).at[token_idx].add(routed_out)
        return out.reshape(bs, slen, dim)
    x = L0_attn_x
    x = _layernorm(x + _L0_attn_ref(x, L0_attn_W_q, L0_attn_W_k, L0_attn_W_v, L0_attn_W_o, L0_attn_gn_weight, L0_attn_gn_bias), axis=-1)
    x = _layernorm(x + _L0_ffn_ref(x, L0_ffn_gate_w, L0_ffn_expert_bias, L0_ffn_w1, L0_ffn_w2, L0_ffn_w3), axis=-1)
    return x

_drawn_inputs = setup_inputs


def setup_inputs(seed=0):
    import zlib

    import numpy as np

    out = dict(_drawn_inputs(seed))
    spreads = {'L0_attn_gn_weight': (1.0, 0.2),
     'L0_attn_gn_bias': (0.0, 0.1),
     'L0_ffn_expert_bias': (0.0, 0.8)}
    factors = {'L0_ffn_gate_w': 8.0, 'L0_ffn_w1': 8.0, 'L0_ffn_w2': 8.0, 'L0_ffn_w3': 8.0}
    for name, (base, spread) in spreads.items():
        noise = np.random.default_rng([zlib.crc32(name.encode()), seed]).standard_normal(out[name].shape)
        drawn = base * np.exp(spread * noise) if base else spread * noise
        out[name] = jnp.asarray(drawn.astype(out[name].dtype))
    for name, factor in factors.items():
        out[name] = (out[name] * factor).astype(out[name].dtype)
    return out
```

```python
import numpy as np
import concourse.bass as bass
from concourse import mybir
from contextlib import ExitStack

B, T, D = 2, 1024, 128
H, DH = 16, 8
NE, TOPK, HID = 8, 2, 352
EPS = 1e-5

P = 128
C = 64
NG = 4
HG = H // NG
PAIRS = T // P
TILES = T * TOPK // P + NE - 1
SLOTS = TILES * P
NT = B * TILES
HC = (HID + P - 1) // P
HP = HC * P

_CONST = [("causal", NG * HG * C), ("ydecay", C), ("kdecay", 2 * D), ("sdecay", 2), ("headsel", HG), ("blockdiag", D),
          ("headmean", D), ("ident", P), ("before", P), ("ones", P), ("rank_e", NE * PAIRS), ("tilestart", NE * NE),
          ("tileid", TILES * NE), ("half", PAIRS)]
COL, _at = {}, 0
for _name, _n in _CONST:
    COL[_name] = (_at, _at + _n)
    _at += _n
NCONST = _at


def shape_constants():
    c = np.zeros((P, NCONST), np.float64)

    def put(name, a):
        c[:, COL[name][0]:COL[name][1]] = np.asarray(a, np.float64).reshape(a.shape[0], -1)

    gamma = 1.0 - 2.0 ** (-5.0 - np.arange(H))
    p = np.arange(P)
    s = p % C
    t = np.arange(C)
    g = gamma.reshape(1, NG, HG, 1)
    put("causal", np.where(t[None, None, None, :] >= s[:, None, None, None], g ** (-(s[:, None, None, None] + 1.0)), 0.0))
    head = p // DH
    put("ydecay", gamma[head][:, None] ** (t[None, :] + 1.0) / np.sqrt(DH))
    k0 = np.where(p[:, None] < C, gamma[head][None, :] ** (C - 1.0 - p[:, None]), 0.0)
    k1 = gamma[head][None, :] ** (2 * C - 1.0 - p[:, None])
    put("kdecay", np.stack([k0, k1], 1))
    put("sdecay", np.stack([gamma[head] ** C, gamma[head] ** (2 * C)], 1))
    put("headsel", (head % HG)[:, None] == np.arange(HG)[None, :])
    same = (head[:, None] == head[None, :]).astype(np.float64)
    put("blockdiag", same)
    put("headmean", same / DH)
    put("ident", np.eye(P))
    put("before", p[:, None] < p[None, :])
    put("ones", np.ones((P, P)))
    put("rank_e", np.broadcast_to(NE - np.arange(NE, dtype=float)[None, None, :], (P, PAIRS, NE)))
    put("tilestart", np.broadcast_to(P * np.arange(NE, dtype=float)[None, None, :], (P, NE, NE)))
    put("tileid", np.broadcast_to(np.arange(TILES, dtype=float)[None, :, None], (P, TILES, NE)))
    put("half", np.full((P, PAIRS), -0.5))
    return c.astype(np.float32)


def retention_moe_kernel(nc, x_tok, x_T, wqT, wkT, wvT, woT, gnw, gnb, gateT, ebias, w1, w2, w3, const, out):
    f32, i32 = mybir.dt.float32, mybir.dt.int32
    ALU = mybir.AluOpType
    ACT = mybir.ActivationFunctionType
    AX = mybir.AxisListType.X

    routed = [nc.dram_tensor(f"routed_rows{b}", [SLOTS, D], f32, kind="Internal").ap() for b in range(B)]
    answers = [nc.dram_tensor(f"expert_rows{b}", [SLOTS, D], f32, kind="Internal").ap() for b in range(B)]

    ctx = ExitStack()
    with ctx:
        def sb(name, shape, dt=f32):
            return ctx.enter_context(nc.sbuf_tensor(name, shape, dt))

        def sem(name):
            return ctx.enter_context(nc.semaphore(name))

        cst = sb("cst", [P, NCONST])

        def const_of(name, rows=P):
            return cst[0:rows, COL[name][0]:COL[name][1]]

        causal = const_of("causal").rearrange("p (g n) -> p g n", g=NG)
        ydecay, kdecay = const_of("ydecay"), const_of("kdecay").rearrange("p (j n) -> p j n", j=2)
        sdecay, headsel = const_of("sdecay"), const_of("headsel")
        blockdiag, headmean, ident = const_of("blockdiag"), const_of("headmean"), const_of("ident")

        wq_s, wk_s, wv_s, wo_s = (sb(n, [P, D]) for n in ("wq_s", "wk_s", "wv_s", "wo_s"))
        gate_s = sb("gate_s", [P, NE])
        gn_s = sb("gn_s", [P, 2])
        eb_s = sb("eb_s", [P, NE])
        w1_s, w3_s = sb("w1_s", [P, NE * HID]), sb("w3_s", [P, NE * HID])
        w2_s = sb("w2_s", [P, NE * HC * D])
        xres = sb("xres", [P, B * PAIRS, D])
        zeros = sb("zeros", [P, D])

        xt = sb("xt", [P, 2, P])
        qT, kT = sb("qT", [P, 2, P]), sb("kT", [P, 2, P])
        qx = sb("qx", [P, 2, HG, P])
        vx = sb("vx", [P, 2, H * 32])
        kd = sb("kd", [P, 2, 2, D])
        att = sb("att", [P, 2, NG, HG * C])
        um = sb("um", [P, 2, D])
        s0, s1 = sb("s0", [P, 2, D]), sb("s1", [P, 2, D])
        yT = sb("yT", [P, T])
        ystats = sb("ystats", [P, PAIRS, 6])
        gn = sb("gn", [P, 12])
        yn = sb("yn", [P, T])

        z = sb("z", [P, PAIRS, D])
        x1 = sb("x1", [P, B * PAIRS, D])
        x1T = sb("x1T", [P, PAIRS, P])
        lstats, lmv = sb("lstats", [P, PAIRS, 6]), sb("lmv", [P, PAIRS, 2])
        lvar, lrstd = sb("lvar", [P, PAIRS]), sb("lrstd", [P, PAIRS])
        rt = {n: sb("rt_" + n, [P, PAIRS, NE]) for n in ("d", "ex", "sc", "key", "eq", "oh1", "oh2", "w")}
        r8 = {n: sb("r8_" + n, [P, PAIRS]) for n in ("mx", "sum", "rc", "m", "f", "tot", "nt", "te", "ts", "off", "sl")}
        prob = sb("prob", [P, TOPK, PAIRS])
        ohe = sb("ohe", [P, NE, PAIRS])
        cum = sb("cum", [P, NE * PAIRS + 1])
        pos = sb("pos", [P, NE, PAIRS])
        gtt = sb("gtt", [P, NE, NE])
        tcmp, tsum = sb("tcmp", [1, TILES, NE]), sb("tsum", [1, TILES])
        slot = sb("slot", [P, B, TOPK, PAIRS], i32)
        expert = sb("expert", [1, NT], i32)
        xs = sb("xs", [P, B, TOPK, PAIRS, D])

        xg, xgT = sb("xg", [P, 2, D]), sb("xgT", [P, 2, P])
        act_s, hid = sb("act_s", [P, 2, HID]), sb("hid", [P, 2, HP])
        hT = sb("hT", [P, 2, HP])
        yo = sb("yo", [P, 2, D])

        bank = [ctx.enter_context(nc.psum_tensor(f"bank{i}", [P, 512], f32)) for i in range(8)]

        s_in = sem("s_in")
        s_xres = sem("s_xres")
        s_moew = sem("s_moew")
        s_zero = sem("s_zero")
        s_blank = sem("s_blank")
        xt_loaded = [sem("xt_loaded0"), sem("xt_loaded1")]
        qkv_done = sem("qkv_done")
        proj_done = sem("proj_done")
        projev_done = sem("projev_done")
        kd_done = sem("kd_done")
        scores_done = sem("scores_done")
        att_done = sem("att_done")
        u_done = sem("u_done")
        um_done = sem("um_done")
        st_done = sem("st_done")
        y_done = sem("y_done")
        yev_done = sem("yev_done")
        yst_done = sem("yst_done")
        dch = sem("dch")
        gnst = sem("gnst")
        gnpe = sem("gnpe")
        var_ready = sem("var_ready")
        rstd_done = sem("rstd_done")
        gnab_done = sem("gnab_done")
        yn_done = sem("yn_done")
        o_done = sem("o_done")
        x1_done = sem("x1_done")
        x1t_pe = sem("x1t_pe")
        x1t_done = sem("x1t_done")
        logit_done = sem("logit_done")
        d_done = sem("d_done")
        exp_done = sem("exp_done")
        oh_done = sem("oh_done")
        rank_done = sem("rank_done")
        prob_done = sem("prob_done")
        slot_done = sem("slot_done")
        xs_done = sem("xs_done")
        scat_done = [sem(f"scat_done{b}") for b in range(B)]
        xg_loaded = [sem("xg_loaded0"), sem("xg_loaded1")]
        t1_done = sem("t1_done")
        xgT_done = sem("xgT_done")
        gate_done = sem("gate_done")
        up_done = sem("up_done")
        silu_done = sem("silu_done")
        hid_done = sem("hid_done")
        t2_done = sem("t2_done")
        hT_done = sem("hT_done")
        down_done = sem("down_done")
        yo_done = sem("yo_done")
        yo_stored = [sem("yo_stored0"), sem("yo_stored1")]
        gath_done = [sem(f"gath_done{b}") for b in range(B)]
        var2_ready = sem("var2_ready")
        rstd2_done = sem("rstd2_done")
        out_ready = sem("out_ready")
        stored = sem("stored")

        N_IN = 9 * 16
        HALF = PAIRS // 2

        block = ctx.enter_context(nc.Block())

        def bcast(ap, n):
            return ap.unsqueeze(2).broadcast_to([ap.shape[0], ap.shape[1], n])

        def vdiag(u):
            v = vx[:, u, :]
            step = v.ap[-1][0]
            return bass.AP(v.tensor, v.offset, [v.ap[0], [P * step, NG], [(32 + DH) * step, HG], [step, DH]])

        @block.sync
        def _(sp):
            def load_pair(p, u):
                sp.dma_start(xt[:, u, :], x_T[:, bass.ds(p * P, P)]).then_inc(xt_loaded[u], 16)

            for dst, src in ((wq_s, wqT), (wk_s, wkT), (wv_s, wvT)):
                sp.dma_start(dst[:, :], src).then_inc(s_in, 16)
            load_pair(0, 0)
            load_pair(1, 1)
            sp.dma_start(cst[:, :], const).then_inc(s_in, 16)
            for dst, src in ((wo_s, woT), (gate_s, gateT), (eb_s, ebias)):
                sp.dma_start(dst[:, :], src).then_inc(s_in, 16)
            sp.dma_start(gn_s[:, 0:1], gnw).then_inc(s_in, 16)
            sp.dma_start(gn_s[:, 1:2], gnb).then_inc(s_in, 16)
            with sp.Fori(0, B * PAIRS // 2 - 1) as i:
                for u in range(2):
                    p = 2 * i + 2 + u
                    sp.wait_ge(proj_done, p - 1)
                    load_pair(p, u)

            def load_tile(b, n, u, reuse=True):
                if reuse:
                    sp.wait_ge(t1_done, b * TILES + n - 1)
                sp.dma_start(xg[:, u, :], routed[b][bass.ds(n * P, P), :]).then_inc(xg_loaded[u], 16)

            def store_tile(b, n, u):
                sp.wait_ge(yo_done, b * TILES + n + 1)
                sp.dma_start(answers[b][bass.ds(n * P, P), :], yo[:, u, :]).then_inc(yo_stored[u], 16)

            LAG = TILES % 2 + 4
            for b in range(B):
                sp.wait_ge(scat_done[b], 16 * TOPK * PAIRS)
                u0 = b * TILES % 2
                for n in range(LAG):
                    load_tile(b, n, (u0 + n) % 2, b > 0 or n > 1)
                    if b:
                        store_tile(b - 1, TILES - LAG + n, (TILES - LAG + n) % 2)
                with sp.Fori(0, (TILES - LAG) // 2) as i:
                    for w in range(2):
                        load_tile(b, 2 * i + LAG + w, (u0 + LAG + w) % 2)
                        store_tile(b, 2 * i + w, (u0 + w) % 2)
            for n in range(TILES - LAG, TILES):
                store_tile(B - 1, n, (u0 + n) % 2)

            for b in range(B):
                for h in range(2):
                    sp.wait_ge(out_ready, 2 * b + h + 1)
                    t0 = b * PAIRS + h * HALF
                    sp.dma_start(out.rearrange("(n p) d -> p n d", p=P)[:, t0:t0 + HALF, :],
                                 z[:, h * HALF:(h + 1) * HALF, :]).then_inc(stored, 16)
            sp.wait_ge(stored, 16 * 2 * B)

        @block.gpsimd
        def _(pool):
            for n, a in enumerate((zeros[:, :], vx[:, :, :], hid[:, :, HID:HP], w2_s[HID - (HC - 1) * P:P, :], cum[:, 0:1])):
                pool.memset(a, 0.0).then_inc(s_zero, 1)
                pool.wait_ge(s_zero, n + 1)
            pool.dma_start(xres[:, :, :], x_tok.rearrange("(n p) d -> p n d", p=P)).then_inc(s_xres, 16)
            pool.wait_ge(s_in, N_IN)

            def rstd(dst, src):
                pool.tensor_tensor(out=dst, in0=src, in1=const_of("half")[:, 0:dst.shape[1]], op=ALU.pow)\
                    .then_inc(rstd_done, 1)

            def scatter(b):
                for k in range(TOPK):
                    for n in range(PAIRS):
                        pool.wait_ge(xs_done, TOPK * PAIRS * b + k * PAIRS + n + 1)
                        pool.indirect_dma_start(
                            out=routed[b][:, :], out_offset=bass.IndirectOffsetOnAxis(ap=slot[:, b, k, n:n + 1], axis=0),
                            in_=xs[:, b, k, n, :], in_offset=None).then_inc(scat_done[b], 16)

            def gather(b):
                for n in range(PAIRS):
                    for k in range(TOPK):
                        pool.indirect_dma_start(
                            out=xs[:, b, k, n, :], out_offset=None, in_=answers[b][:, :],
                            in_offset=bass.IndirectOffsetOnAxis(ap=slot[:, b, k, n:n + 1], axis=0))\
                            .then_inc(gath_done[b], 16)

            for b in range(B):
                pool.wait_ge(var_ready, 2 * b + 1)
                rstd(gn[:, 6:7], gn[:, 5:6])
                pool.wait_ge(var_ready, 2 * b + 2)
                rstd(lrstd[:, :], lvar[:, :])
                pool.wait_ge(slot_done, b + 1)
                if b == 0:
                    pool.wait_ge(s_blank, 16 * B)
                scatter(b)
            for b in range(B):
                last = (b + 1) * TILES
                pool.wait_ge(yo_stored[0], 16 * ((last + 1) // 2))
                pool.wait_ge(yo_stored[1], 16 * (last // 2))
                pool.wait_ge(scat_done[b], 16 * TOPK * PAIRS)
                gather(b)
            for b in range(B):
                pool.wait_ge(var_ready, 2 * B + b + 1)
                rstd(lrstd[:, :], lvar[:, :])

        @block.scalar
        def _(act):
            act.wait_ge(s_zero, 5)
            for b in range(B):
                act.dma_start(routed[b].rearrange("(n p) d -> p n d", p=P),
                              zeros[:, :].unsqueeze(1).broadcast_to([P, TILES, D])).then_inc(s_blank, 16)
            act.dma_start(w1_s[:, :].rearrange("p (e n) -> p e n", e=NE), w1.rearrange("e p n -> p e n")).then_inc(s_moew, 16)
            act.dma_start(w3_s[:, :].rearrange("p (e n) -> p e n", e=NE), w3.rearrange("e p n -> p e n")).then_inc(s_moew, 16)
            w2v = w2_s[:, :].rearrange("p (e c n) -> p e c n", e=NE, c=HC)
            for c in range(HC):
                rows = min(P, HID - c * P)
                act.dma_start(w2v[0:rows, :, c, :], w2[:, c * P:c * P + rows, :].rearrange("e p n -> p e n"))\
                    .then_inc(s_moew, 16)
            act.wait_ge(s_in, N_IN)

            def evacuate(p, u, reuse=True):
                act.wait_ge(qkv_done, p + 1)
                if reuse:
                    act.wait_ge(y_done, p - 1)
                nc.scalar.copy(qT[:, u, :], bank[0][:, 0:P])
                nc.scalar.copy(kT[:, u, :], bank[0][:, P:2 * P])
                nc.scalar.copy(vdiag(u), bank[0][:, 2 * P:3 * P].rearrange("p (g i d) -> p g i d", g=NG, i=HG))
                for i in range(HG):
                    last = nc.scalar.activation(qx[:, u, i, :], bank[0][:, 0:P], ACT.Copy, scale=headsel[:, i:i + 1])
                last.then_inc(projev_done, 1)

            for b in range(B):
                base = b * PAIRS
                evacuate(base, 0, b > 0)
                evacuate(base + 1, 1, b > 0)
                with act.Fori(0, PAIRS // 2 - 1) as i:
                    for u in range(2):
                        evacuate(base + 2 + 2 * i + u, u)

                act.wait_ge(gnab_done, b + 1)
                if b > 0:
                    act.wait_ge(o_done, 2 * b)
                for h in range(2):
                    nc.scalar.activation(yn[:, h * 512:(h + 1) * 512], yT[:, h * 512:(h + 1) * 512], ACT.Identity,
                                         scale=gn[:, 7:8], bias=gn[:, 9:10]).then_inc(yn_done, 1)
                for h in range(2):
                    act.wait_ge(x1t_pe, 2 * b + h + 1)
                    if b > 0 and h == 0:
                        act.wait_ge(logit_done, b)
                    nc.scalar.copy(x1T[:, h * HALF:(h + 1) * HALF, :],
                                   bank[4 + h][:, :].rearrange("p (n d) -> p n d", n=HALF)).then_inc(x1t_done, 1)
                act.wait_ge(d_done, b + 1)
                nc.scalar.activation(rt["ex"][:, :, :], rt["d"][:, :, :], ACT.Exp).then_inc(exp_done, 1)
                act.wait_ge(prob_done, b + 1)
                for k in range(TOPK):
                    for n in range(PAIRS):
                        nc.scalar.activation(xs[:, b, k, n, :], x1[:, b * PAIRS + n, :], ACT.Copy,
                                             scale=prob[:, k, n:n + 1]).then_inc(xs_done, 1)

            def silu(g, u, reuse=True):
                act.wait_ge(gate_done, g + 1)
                if reuse:
                    act.wait_ge(hid_done, g - 1)
                nc.scalar.activation(act_s[:, u, :], bank[1 + u][:, 0:HID], ACT.Silu).then_inc(silu_done, 1)

            def hidden_T(g, u, reuse=True):
                act.wait_ge(t2_done, g + 1)
                if reuse:
                    act.wait_ge(down_done, g - 1)
                nc.scalar.copy(hT[:, u, :], bank[5][:, 0:HP]).then_inc(hT_done, 1)

            silu(0, 0, False)
            silu(1, 1, False)
            hidden_T(0, 0, False)
            silu(2, 0)
            hidden_T(1, 1, False)
            with act.Fori(0, (NT - 4) // 2) as i:
                for u in range(2):
                    g = 2 * i + 3 + u
                    silu(g, (3 + u) % 2)
                    hidden_T(g - 1, u % 2)
            silu(NT - 1, 1)
            hidden_T(NT - 2, 0)
            hidden_T(NT - 1, 1)

        @block.vector
        def _(dve):
            chain = [0]

            def link(ins):
                chain[0] += 1
                ins.then_inc(dch, 1)
                dve.wait_ge(dch, chain[0])

            V = nc.vector

            def decay_k(p, u):
                dve.wait_ge(proj_done, p + 1)
                V.tensor_tensor(out=kd[:, u, :, :], in0=bank[1][:, 0:D].unsqueeze(1).broadcast_to([P, 2, D]),
                                in1=kdecay, op=ALU.mult).then_inc(kd_done, 1)

            def decay_scores(p, u):
                for half in range(2):
                    dve.wait_ge(scores_done, 2 * p + half + 1)
                    for g in (2 * half, 2 * half + 1):
                        ins = V.tensor_tensor(out=att[:, u, g, :], in0=bank[2 + g][:, 0:HG * C],
                                              in1=causal[:, g, :], op=ALU.mult)
                    ins.then_inc(att_done, 1)

            def states(p, u):
                dve.wait_ge(u_done, p + 1)
                V.tensor_tensor(out=um[:, :, :], in0=bank[1][:, P:3 * P].rearrange("p (j n) -> p j n", j=2),
                                in1=blockdiag.unsqueeze(1).broadcast_to([P, 2, D]), op=ALU.mult).then_inc(um_done, 1)
                dve.wait_ge(um_done, p + 1)
                dve.wait_ge(y_done, p)
                V.scalar_tensor_tensor(out=s1[:, u, :], in0=s0[:, u, :], scalar=sdecay[:, 0:1], in1=um[:, 0, :],
                                       op0=ALU.mult, op1=ALU.add)
                V.scalar_tensor_tensor(out=s0[:, 1 - u, :], in0=s0[:, u, :], scalar=sdecay[:, 1:2], in1=um[:, 1, :],
                                       op0=ALU.mult, op1=ALU.add).then_inc(st_done, 1)
                dve.wait_ge(st_done, p + 1)

            def evacuate_y(p, local):
                dve.wait_ge(y_done, p + 1)
                for j in range(2):
                    ins = V.tensor_tensor(out=yT[:, bass.ds(local * P + j * C, C)], in0=bank[6 + j][:, 0:C], in1=ydecay,
                                          op=ALU.mult)
                ins.then_inc(yev_done, 1)
                dve.wait_ge(yev_done, p + 1)
                V.bn_stats(out=ystats[:, local, :] if isinstance(local, int) else
                           ystats[:, :, :].rearrange("p n s -> p (n s)")[:, bass.ds(local * 6, 6)],
                           in_=yT[:, bass.ds(local * P, P)]).then_inc(yst_done, 1)

            def layer_norm(dst, n_var, half_done):
                for n in range(PAIRS):
                    ins = V.bn_stats(out=lstats[:, n, :], in_=z[:, n, :])
                link(ins)
                for n in range(PAIRS):
                    ins = V.bn_aggr(out=lmv[:, n, :], in_=lstats[:, n, :])
                link(ins)
                V.tensor_scalar(lvar[:, :], lmv[:, :, 1], EPS, None, ALU.add).then_inc(var_ready, 1)
                dve.wait_ge(rstd_done, n_var)
                for h in range(2):
                    for n in range(h * HALF, (h + 1) * HALF):
                        ins = V.tensor_scalar(dst(n), z[:, n, :], lmv[:, n, 0:1], lrstd[:, n:n + 1],
                                              ALU.subtract, ALU.mult)
                    ins.then_inc(half_done, 1)

            dve.wait_ge(s_in, N_IN)
            dve.wait_ge(s_zero, 5)
            for b in range(B):
                base = b * PAIRS
                link(V.memset(s0[:, 0, :], 0.0))
                decay_k(base, 0)
                decay_scores(base, 0)
                states(base, 0)
                decay_k(base + 1, 1)
                with dve.Fori(0, PAIRS // 2 - 1) as i:
                    for w in range(2):
                        p, u = 2 * i + 1 + w, (1 + w) % 2
                        decay_scores(base + p, u)
                        states(base + p, u)
                        evacuate_y(base + p - 1, p - 1)
                        decay_k(base + p + 1, 1 - u)
                decay_scores(base + PAIRS - 1, 1)
                states(base + PAIRS - 1, 1)
                evacuate_y(base + PAIRS - 2, PAIRS - 2)
                evacuate_y(base + PAIRS - 1, PAIRS - 1)

                dve.wait_ge(yst_done, base + PAIRS)
                V.bn_aggr(out=gn[:, 0:2], in_=ystats[:, :, :].rearrange("p n s -> p (n s)")).then_inc(gnst, 1)
                dve.wait_ge(gnpe, 2 * b + 1)
                link(V.tensor_copy(gn[:, 2:4], bank[1][:, 0:2]))
                link(V.tensor_tensor(out=gn[:, 11:12], in0=gn[:, 0:1], in1=gn[:, 2:3], op=ALU.subtract))
                V.tensor_tensor(out=gn[:, 4:5], in0=gn[:, 11:12], in1=gn[:, 11:12], op=ALU.mult).then_inc(gnst, 1)
                dve.wait_ge(gnpe, 2 * b + 2)
                V.scalar_tensor_tensor(out=gn[:, 5:6], in0=bank[1][:, 2:3], scalar=EPS, in1=gn[:, 3:4],
                                       op0=ALU.add, op1=ALU.add).then_inc(var_ready, 1)
                dve.wait_ge(rstd_done, 2 * b + 1)
                link(V.tensor_tensor(out=gn[:, 7:8], in0=gn[:, 6:7], in1=gn_s[:, 0:1], op=ALU.mult))
                link(V.tensor_tensor(out=gn[:, 8:9], in0=gn[:, 2:3], in1=gn[:, 7:8], op=ALU.mult))
                V.tensor_tensor(out=gn[:, 9:10], in0=gn_s[:, 1:2], in1=gn[:, 8:9], op=ALU.subtract).then_inc(gnab_done, 1)

                dve.wait_ge(s_xres, 16)
                for h in range(2):
                    dve.wait_ge(o_done, 2 * b + h + 1)
                    t0 = base + h * HALF
                    ins = V.tensor_tensor(out=z[:, h * HALF:(h + 1) * HALF, :],
                                          in0=bank[2 + h][:, :].rearrange("p (n d) -> p n d", n=HALF),
                                          in1=xres[:, t0:t0 + HALF, :], op=ALU.add)
                link(ins)
                layer_norm(lambda n: x1[:, base + n, :], 2 * b + 2, x1_done)

                t3 = {n: a[:, :, :] for n, a in rt.items()}
                logits = bank[0][:, 0:PAIRS * NE].rearrange("p (n e) -> p n e", e=NE)
                desc = const_of("rank_e").rearrange("p (n e) -> p n e", e=NE)
                dve.wait_ge(logit_done, b + 1)
                link(V.tensor_reduce(r8["mx"][:, :], logits, AX, ALU.max))
                V.tensor_tensor(out=t3["d"], in0=logits, in1=bcast(r8["mx"][:, :], NE), op=ALU.subtract).then_inc(d_done, 1)
                dve.wait_ge(exp_done, b + 1)
                link(V.tensor_reduce(r8["sum"][:, :], t3["ex"], AX, ALU.add))
                link(V.reciprocal(r8["rc"][:, :], r8["sum"][:, :]))
                link(V.tensor_tensor(out=t3["sc"], in0=t3["ex"], in1=bcast(r8["rc"][:, :], NE), op=ALU.mult))
                link(V.tensor_tensor(out=t3["key"], in0=t3["sc"],
                                     in1=eb_s[:, :].unsqueeze(1).broadcast_to([P, PAIRS, NE]), op=ALU.add))
                for k in range(TOPK):
                    oh = t3[f"oh{k + 1}"]
                    link(V.tensor_reduce(r8["m"][:, :], t3["key"], AX, ALU.max))
                    link(V.tensor_tensor(out=t3["eq"], in0=t3["key"], in1=bcast(r8["m"][:, :], NE), op=ALU.is_equal))
                    link(V.tensor_tensor(out=t3["w"], in0=t3["eq"], in1=desc, op=ALU.mult))
                    link(V.tensor_reduce(r8["f"][:, :], t3["w"], AX, ALU.max))
                    link(V.tensor_tensor(out=oh, in0=desc, in1=bcast(r8["f"][:, :], NE), op=ALU.is_equal))
                    if k == 0:
                        link(V.scalar_tensor_tensor(out=t3["key"], in0=oh, scalar=-3e38, in1=t3["key"],
                                                    op0=ALU.mult, op1=ALU.add))
                V.tensor_tensor(out=ohe[:, :, :].rearrange("p e n -> p n e"), in0=t3["oh1"], in1=t3["oh2"],
                                op=ALU.add).then_inc(oh_done, 1)
                for k in range(TOPK):
                    link(V.tensor_tensor(out=t3["w"], in0=t3["sc"], in1=t3[f"oh{k + 1}"], op=ALU.mult))
                    ins = V.tensor_reduce(prob[:, k, :], t3["w"], AX, ALU.add)
                    if k == 0:
                        link(ins)
                ins.then_inc(prob_done, 1)
                n64 = NE * PAIRS
                within, counts = bank[1][:, 0:n64], bank[1][:, n64:2 * n64]
                dve.wait_ge(rank_done, b + 1)
                link(V.tensor_tensor_scan(cum[:, 1:n64 + 1], const_of("ones")[:, 0:n64], counts, 0.0, ALU.mult, ALU.add))
                link(V.tensor_tensor(out=pos[:, :, :].rearrange("p e n -> p (e n)"), in0=cum[:, 1:n64 + 1], in1=counts,
                                     op=ALU.subtract))
                starts, ends = cum[:, 0:n64:PAIRS], cum[:, PAIRS:n64 + 1:PAIRS]
                link(V.tensor_tensor(out=r8["tot"][:, :], in0=ends, in1=starts, op=ALU.subtract))
                link(V.tensor_tensor(out=gtt[:, :, :], in0=bcast(r8["tot"][:, :], NE),
                                     in1=const_of("tilestart").rearrange("p (e j) -> p e j", j=NE), op=ALU.is_gt))
                link(V.tensor_reduce(r8["nt"][:, :], gtt[:, :, :], AX, ALU.add))
                link(V.tensor_tensor_scan(r8["te"][:, :], const_of("ones")[:, 0:NE], r8["nt"][:, :], 0.0, ALU.mult, ALU.add))
                link(V.tensor_tensor(out=r8["ts"][:, :], in0=r8["te"][:, :], in1=r8["nt"][:, :], op=ALU.subtract))
                link(V.scalar_tensor_tensor(out=r8["off"][:, :], in0=r8["ts"][:, :], scalar=float(P), in1=starts,
                                            op0=ALU.mult, op1=ALU.subtract))
                link(V.tensor_tensor(out=pos[:, :, :], in0=pos[:, :, :], in1=bcast(r8["off"][:, :], PAIRS), op=ALU.add))
                link(V.tensor_tensor(out=pos[:, :, :].rearrange("p e n -> p (e n)"),
                                     in0=pos[:, :, :].rearrange("p e n -> p (e n)"), in1=within, op=ALU.add))
                for k in range(TOPK):
                    link(V.tensor_tensor(out=t3["w"], in0=t3[f"oh{k + 1}"], in1=pos[:, :, :].rearrange("p e n -> p n e"),
                                         op=ALU.mult))
                    link(V.tensor_reduce(r8["sl"][:, :], t3["w"], AX, ALU.add))
                    link(V.tensor_copy(slot[:, b, k, :], r8["sl"][:, :]))
                link(V.tensor_tensor(out=tcmp[:, :, :], in0=const_of("tileid", 1).rearrange("p (g e) -> p g e", e=NE),
                                     in1=r8["te"][0:1, :].unsqueeze(1).broadcast_to([1, TILES, NE]), op=ALU.is_ge))
                link(V.tensor_reduce(tsum[:, :], tcmp[:, :, :], AX, ALU.add))
                V.tensor_scalar(expert[:, b * TILES:(b + 1) * TILES], tsum[:, :], float(NE - 1), None, ALU.min)\
                    .then_inc(slot_done, 1)

            def rows_T(g, u):
                dve.wait_ge(t1_done, g + 1)
                V.tensor_copy(xgT[:, u, :], bank[0][:, 0:P]).then_inc(xgT_done, 1)

            def hidden(g, u, reuse=True):
                dve.wait_ge(silu_done, g + 1)
                dve.wait_ge(up_done, g + 1)
                if reuse:
                    dve.wait_ge(t2_done, g - 1)
                V.tensor_tensor(out=hid[:, u, 0:HID], in0=bank[3 + u][:, 0:HID], in1=act_s[:, u, :], op=ALU.mult)\
                    .then_inc(hid_done, 1)

            def answer(g, u, slot_wait):
                dve.wait_ge(down_done, g + 1)
                if slot_wait is not None:
                    dve.wait_ge(yo_stored[u], slot_wait)
                V.tensor_copy(yo[:, u, :], bank[6][:, 0:D]).then_inc(yo_done, 1)

            rows_T(0, 0)
            rows_T(1, 1)
            hidden(0, 0, False)
            rows_T(2, 0)
            hidden(1, 1, False)
            for g in (2, 3):
                rows_T(g + 1, (g + 1) % 2)
                answer(g - 2, g % 2, None)
                hidden(g, g % 2)
            with dve.Fori(0, (NT - 6) // 2) as i:
                for u in range(2):
                    g = 2 * i + 4 + u
                    rows_T(g + 1, 1 - u)
                    answer(g - 2, u, 16 * (i + 1))
                    hidden(g, u)
            rows_T(NT - 1, 1)
            answer(NT - 4, 0, 16 * (NT // 2 - 2))
            hidden(NT - 2, 0)
            answer(NT - 3, 1, 16 * (NT // 2 - 2))
            hidden(NT - 1, 1)
            answer(NT - 2, 0, 16 * (NT // 2 - 1))
            answer(NT - 1, 1, 16 * (NT // 2 - 1))

            for b in range(B):
                dve.wait_ge(gath_done[b], 16 * TOPK * PAIRS)
                if b > 0:
                    dve.wait_ge(stored, 16 * 2 * b)
                link(V.tensor_tensor(out=z[:, :, :], in0=xs[:, b, 0, :, :], in1=xs[:, b, 1, :, :], op=ALU.add))
                link(V.tensor_tensor(out=z[:, :, :], in0=z[:, :, :], in1=x1[:, b * PAIRS:(b + 1) * PAIRS, :], op=ALU.add))
                layer_norm(lambda n: z[:, n, :], 2 * B + b + 1, out_ready)

        @block.tensor
        def _(pe):
            MM = nc.tensor.matmul
            pe.wait_ge(s_in, N_IN)
            pe.wait_ge(s_zero, 5)

            def project(p, u, n_loaded):
                x = xt[:, u, :]
                pe.wait_ge(xt_loaded[u], n_loaded)
                pe.wait_ge(projev_done, p)
                MM(bank[0][:, 0:P], wq_s[:, :], x, start=True, stop=True)
                MM(bank[0][:, P:2 * P], wk_s[:, :], x, start=True, stop=True)
                MM(bank[0][:, 2 * P:3 * P], x, wv_s[:, :], start=True, stop=True).then_inc(qkv_done, 1)
                pe.wait_ge(um_done, p)
                MM(bank[1][:, 0:D], x, wk_s[:, :], start=True, stop=True).then_inc(proj_done, 1)

            def scores(p, u):
                pe.wait_ge(projev_done, p + 1)
                for half in range(2):
                    for j, gg in ((0, 0), (1, 1), (1, 0), (0, 1)):
                        g = 2 * half + gg
                        r = slice(32 * g, 32 * g + 32)
                        c = slice(C * j, C * j + C)
                        last = MM(bank[2 + g][c, 0:HG * C], kT[r, u, c], qx[r, u, :, c], start=True, stop=True)
                    last.then_inc(scores_done, 1)

            def increments(p, u):
                pe.wait_ge(kd_done, p + 1)
                for j in range(2):
                    last = MM(bank[1][:, (1 + j) * P:(2 + j) * P], kd[:, u, j, :], vdiag(u), start=True, stop=True)
                last.then_inc(u_done, 1)

            def outputs(p, u):
                pe.wait_ge(att_done, 2 * p + 2)
                pe.wait_ge(st_done, p + 1)
                pe.wait_ge(yev_done, p)
                for j, s in enumerate((s0, s1)):
                    MM(bank[6 + j][:, 0:C], s[:, u, :], qT[:, u, C * j:C * j + C], start=True, stop=False,
                       skip_group_check=True)
                for i in range(HG):
                    for g in range(NG):
                        for j in range(2):
                            c = slice(C * j, C * j + C)
                            h = g * HG + i
                            last = MM(bank[6 + j][32 * g:32 * g + 32, 0:C],
                               vx[c, u, 32 * h:32 * h + 32],
                               att[c, u, g, i * C:(i + 1) * C], start=False, stop=i == HG - 1, skip_group_check=True)
                last.then_inc(y_done, 1)

            for b in range(B):
                base = b * PAIRS
                if b:
                    pe.wait_ge(slot_done, b)
                project(base, 0, 16 * (base // 2 + 1))
                scores(base, 0)
                increments(base, 0)
                project(base + 1, 1, 16 * (base // 2 + 1))
                outputs(base, 0)
                with pe.Fori(0, PAIRS // 2 - 1) as i:
                    for w in range(2):
                        p, u = base + 2 * i + 1 + w, (1 + w) % 2
                        scores(p, u)
                        increments(p, u)
                        project(p + 1, 1 - u, 16 * (base // 2 + i + 2))
                        outputs(p, u)
                scores(base + PAIRS - 1, 1)
                increments(base + PAIRS - 1, 1)
                outputs(base + PAIRS - 1, 1)

                pe.wait_ge(um_done, base + PAIRS)
                pe.wait_ge(gnst, 2 * b + 1)
                MM(bank[1][:, 0:2], headmean, gn[:, 0:2], start=True, stop=True).then_inc(gnpe, 1)
                pe.wait_ge(gnst, 2 * b + 2)
                MM(bank[1][:, 2:3], headmean, gn[:, 4:5], start=True, stop=True).then_inc(gnpe, 1)

                for h in range(2):
                    pe.wait_ge(yn_done, 2 * b + h + 1)
                    for n in range(HALF):
                        t0 = (h * HALF + n) * P
                        last = MM(bank[2 + h][:, n * D:(n + 1) * D], yn[:, t0:t0 + P], wo_s[:, :], start=True, stop=True)
                    last.then_inc(o_done, 1)
                for h in range(2):
                    pe.wait_ge(x1_done, 2 * b + h + 1)
                    for n in range(HALF):
                        last = nc.tensor.transpose(bank[4 + h][:, n * P:(n + 1) * P], x1[:, base + h * HALF + n, :], ident)
                    last.then_inc(x1t_pe, 1)
                for h in range(2):
                    pe.wait_ge(x1t_done, 2 * b + h + 1)
                    for n in range(h * HALF, (h + 1) * HALF):
                        last = MM(bank[0][:, n * NE:(n + 1) * NE], x1T[:, n, :], gate_s[:, :], start=True, stop=True)
                last.then_inc(logit_done, 1)
                pe.wait_ge(oh_done, b + 1)
                n64 = NE * PAIRS
                o = ohe[:, :, :].rearrange("p e n -> p (e n)")
                MM(bank[1][:, 0:n64], const_of("before"), o, start=True, stop=True)
                MM(bank[1][:, n64:2 * n64], const_of("ones"), o, start=True, stop=True).then_inc(rank_done, 1)

            def expert_of(g):
                return pe.value_load(expert[0:1, bass.ds(g, 1)], min_val=0, max_val=NE - 1)

            def transpose_rows(g, u, n_loaded):
                pe.wait_ge(xg_loaded[u], n_loaded)
                pe.wait_ge(xgT_done, g)
                nc.tensor.transpose(bank[0][:, 0:P], xg[:, u, :], ident).then_inc(t1_done, 1)

            def gate_up(g, u, reuse=True):
                e = expert_of(g)
                pe.wait_ge(xgT_done, g + 1)
                if reuse:
                    pe.wait_ge(hid_done, g - 1)
                MM(bank[1 + u][:, 0:HID], xgT[:, u, :], w1_s[:, bass.ds(e * HID, HID)], start=True, stop=True)\
                    .then_inc(gate_done, 1)
                MM(bank[3 + u][:, 0:HID], xgT[:, u, :], w3_s[:, bass.ds(e * HID, HID)], start=True, stop=True)\
                    .then_inc(up_done, 1)

            def transpose_hidden(g, u):
                pe.wait_ge(hid_done, g + 1)
                pe.wait_ge(hT_done, g)
                for c in range(HC):
                    last = nc.tensor.transpose(bank[5][:, c * P:(c + 1) * P], hid[:, u, c * P:(c + 1) * P], ident)
                last.then_inc(t2_done, 1)

            def down(g, u, reuse=True):
                e = expert_of(g)
                pe.wait_ge(hT_done, g + 1)
                if reuse:
                    pe.wait_ge(yo_done, g)
                for c in range(HC):
                    last = MM(bank[6][:, 0:D], hT[:, u, c * P:(c + 1) * P], w2_s[:, bass.ds(e * (HC * D) + c * D, D)],
                              start=c == 0, stop=c == HC - 1)
                last.then_inc(down_done, 1)

            pe.wait_ge(s_moew, 16 * (2 + HC))
            pe.wait_ge(slot_done, B)
            transpose_rows(0, 0, 16)
            transpose_rows(1, 1, 16)
            gate_up(0, 0, False)
            transpose_rows(2, 0, 32)
            gate_up(1, 1, False)
            transpose_hidden(0, 0)
            for g in (2, 3):
                transpose_rows(g + 1, 1 - g % 2, 16 * ((g + 1) // 2 + 1))
                gate_up(g, g % 2)
                down(g - 2, g % 2, g > 2)
                transpose_hidden(g - 1, 1 - g % 2)
            with pe.Fori(0, (NT - 6) // 2) as i:
                for u in range(2):
                    g = 2 * i + 4 + u
                    transpose_rows(g + 1, 1 - u, 16 * (i + 3 + u))
                    gate_up(g, u)
                    down(g - 2, u)
                    transpose_hidden(g - 1, 1 - u)
            transpose_rows(NT - 1, 1, 16 * (NT // 2))
            gate_up(NT - 2, 0)
            down(NT - 4, 0)
            transpose_hidden(NT - 3, 1)
            gate_up(NT - 1, 1)
            down(NT - 3, 1)
            transpose_hidden(NT - 2, 0)
            down(NT - 2, 0)
            transpose_hidden(NT - 1, 1)
            down(NT - 1, 1)


def kernel(L0_attn_x, L0_attn_W_q, L0_attn_W_k, L0_attn_W_v, L0_attn_W_o, L0_attn_gn_weight, L0_attn_gn_bias,
           L0_ffn_gate_w, L0_ffn_expert_bias, L0_ffn_w1, L0_ffn_w2, L0_ffn_w3):
    import concourse.bacc as bacc
    from concourse.bass_utils import run_bass_kernel_spmd

    def lay(a):
        return np.ascontiguousarray(a)

    x = np.asarray(L0_attn_x).reshape(B * T, D)
    arrays = {
        "x_tok": lay(x), "x_T": lay(x.T),
        "wqT": lay(np.asarray(L0_attn_W_q).T), "wkT": lay(np.asarray(L0_attn_W_k).T),
        "wvT": lay(np.asarray(L0_attn_W_v).T), "woT": lay(np.asarray(L0_attn_W_o).T),
        "gnw": lay(np.asarray(L0_attn_gn_weight).reshape(D, 1)), "gnb": lay(np.asarray(L0_attn_gn_bias).reshape(D, 1)),
        "gateT": lay(np.asarray(L0_ffn_gate_w).T),
        "ebias": lay(np.broadcast_to(np.asarray(L0_ffn_expert_bias)[None, :], (P, NE))),
        "w1": lay(L0_ffn_w1), "w2": lay(L0_ffn_w2), "w3": lay(L0_ffn_w3),
        "const": shape_constants(),
    }
    nc = bacc.Bacc("TRN2", target_bir_lowering=False, num_devices=1)
    args = [nc.dram_tensor(f"in_{n}", a.shape, mybir.dt.from_np(a.dtype), kind="ExternalInput").ap()
            for n, a in arrays.items()]
    args.append(nc.dram_tensor("out_0", (B * T, D), mybir.dt.float32, kind="ExternalOutput").ap())
    retention_moe_kernel(nc, *args)
    r = run_bass_kernel_spmd(nc, [{f"in_{n}": a for n, a in arrays.items()}], core_ids=[0])
    return r.results[0]["out_0"].reshape(B, T, D)
```

```python
import numpy as np
import concourse.bass as bass
from concourse import mybir
from contextlib import ExitStack

B, T, D = 2, 1024, 128
H, DH = 16, 8
NE, TOPK, HID = 8, 2, 352
EPS = 1e-5

P = 128
C = 64
NG = 4
HG = H // NG
PAIRS = T // P
TILES = T * TOPK // P + NE - 1
SLOTS = TILES * P
WCOLS = 2 * HID + (HID + P - 1) // P * D
NT = B * TILES
HC = (HID + P - 1) // P
HP = HC * P

ROUTED = 14
COMBINED = 34

_CONST = [("causal", NG * HG * C), ("ydecay", C), ("kdecay", 2 * D), ("sdecay", 2), ("headsel", HG), ("blockdiag", D),
          ("headmean", D), ("ident", P), ("before", P), ("ones", P), ("rank_e", NE * PAIRS), ("tilestart", NE * NE),
          ("tileid", TILES * NE), ("half", PAIRS)]
COL, _at = {}, 0
for _name, _n in _CONST:
    COL[_name] = (_at, _at + _n)
    _at += _n
NCONST = _at


def shape_constants():
    c = np.zeros((P, NCONST), np.float64)

    def put(name, a):
        c[:, COL[name][0]:COL[name][1]] = np.asarray(a, np.float64).reshape(a.shape[0], -1)

    gamma = 1.0 - 2.0 ** (-5.0 - np.arange(H))
    p = np.arange(P)
    s = p % C
    t = np.arange(C)
    g = gamma.reshape(1, NG, HG, 1)
    put("causal", np.where(t[None, None, None, :] >= s[:, None, None, None], g ** (-(s[:, None, None, None] + 1.0)), 0.0))
    head = p // DH
    put("ydecay", gamma[head][:, None] ** (t[None, :] + 1.0) / np.sqrt(DH))
    k0 = np.where(p[:, None] < C, gamma[head][None, :] ** (C - 1.0 - p[:, None]), 0.0)
    k1 = gamma[head][None, :] ** (2 * C - 1.0 - p[:, None])
    put("kdecay", np.stack([k0, k1], 1))
    put("sdecay", np.stack([gamma[head] ** C, gamma[head] ** (2 * C)], 1))
    put("headsel", (head % HG)[:, None] == np.arange(HG)[None, :])
    same = (head[:, None] == head[None, :]).astype(np.float64)
    put("blockdiag", same)
    put("headmean", same / DH)
    put("ident", np.eye(P))
    put("before", p[:, None] < p[None, :])
    put("ones", np.ones((P, P)))
    put("rank_e", np.broadcast_to(NE - np.arange(NE, dtype=float)[None, None, :], (P, PAIRS, NE)))
    put("tilestart", np.broadcast_to(P * np.arange(NE, dtype=float)[None, None, :], (P, NE, NE)))
    put("tileid", np.broadcast_to(np.arange(TILES, dtype=float)[None, :, None], (P, TILES, NE)))
    put("half", np.full((P, PAIRS), -0.5))
    return c.astype(np.float32)


def retention_moe_kernel(nc, x_tok, x_T, wqT, wkT, wvT, woT, gnw, gnb, gateT, ebias, w1, w2, w3, const, out):
    f32, i32 = mybir.dt.float32, mybir.dt.int32
    ALU = mybir.AluOpType
    ACT = mybir.ActivationFunctionType
    AX = mybir.AxisListType.X

    routed = [nc.dram_tensor(f"routed_rows{b}", [SLOTS, D], f32, kind="Internal").ap() for b in range(B)]
    answers = [nc.dram_tensor(f"expert_rows{b}", [SLOTS, D], f32, kind="Internal").ap() for b in range(B)]

    ctx = ExitStack()
    with ctx:
        def sb(name, shape, dt=f32):
            return ctx.enter_context(nc.sbuf_tensor(name, shape, dt))

        def sem(name):
            return ctx.enter_context(nc.semaphore(name))

        cst = sb("cst", [P, NCONST])

        def const_of(name, rows=P):
            return cst[0:rows, COL[name][0]:COL[name][1]]

        causal = const_of("causal").rearrange("p (g n) -> p g n", g=NG)
        ydecay, kdecay = const_of("ydecay"), const_of("kdecay").rearrange("p (j n) -> p j n", j=2)
        sdecay, headsel = const_of("sdecay"), const_of("headsel")
        blockdiag, headmean, ident = const_of("blockdiag"), const_of("headmean"), const_of("ident")

        wq_s, wk_s, wv_s, wo_s = (sb(n, [P, D]) for n in ("wq_s", "wk_s", "wv_s", "wo_s"))
        gate_s = sb("gate_s", [P, NE])
        gn_s = sb("gn_s", [P, 2])
        eb_s = sb("eb_s", [P, NE])
        w_s = sb("w_s", [P, NE, WCOLS])
        xres = sb("xres", [P, B * PAIRS, D])
        zeros = sb("zeros", [P, D])

        warm = sb("warm", [P, 512], mybir.dt.bfloat16)

        xT_all = sb("xT_all", [P, B * T])
        xt = sb("xt", [P, 2, P])
        qT, kT = sb("qT", [P, 2, P]), sb("kT", [P, 2, P])
        qx = sb("qx", [P, 2, HG, P])
        vx = sb("vx", [P, 2, H * 32])
        kd = sb("kd", [P, 2, 2, D])
        att = sb("att", [P, 2, NG, HG * C])
        um = sb("um", [P, 2, D])
        s0, s1 = sb("s0", [P, 2, D]), sb("s1", [P, 2, D])
        yT = sb("yT", [P, B * T])
        ystats = sb("ystats", [P, B * PAIRS, 6])
        gn = sb("gn", [P, 12])
        yn = sb("yn", [P, T])

        z = sb("z", [P, B * PAIRS, D])
        x1 = sb("x1", [P, B * PAIRS, D])
        x1T = sb("x1T", [P, PAIRS, P])
        lstats, lmv = sb("lstats", [P, PAIRS, 6]), sb("lmv", [P, PAIRS, 2])
        lvar, lrstd = sb("lvar", [P, PAIRS]), sb("lrstd", [P, PAIRS])
        rt = {n: sb("rt_" + n, [P, PAIRS, NE]) for n in ("d", "ex", "sc", "key", "eq", "oh1", "oh2", "w")}
        r8 = {n: sb("r8_" + n, [P, PAIRS]) for n in ("mx", "sum", "rc", "m", "f", "tot", "nt", "te", "ts", "off", "sl")}
        prob = sb("prob", [P, TOPK, PAIRS])
        ohe = sb("ohe", [P, NE, PAIRS])
        rank = sb("rank", [P, 2 * NE * PAIRS])
        cum = sb("cum", [P, NE * PAIRS + 1])
        pos = sb("pos", [P, NE, PAIRS])
        gtt = sb("gtt", [P, NE, NE])
        tcmp, tsum = sb("tcmp", [1, TILES, NE]), sb("tsum", [1, TILES])
        slot = sb("slot", [P, B, TOPK, PAIRS], i32)
        expert = sb("expert", [1, NT], i32)
        xs = sb("xs", [P, B, TOPK, PAIRS, D])

        xg, xgT = sb("xg", [P, 2, D]), sb("xgT", [P, 2, P])
        act_s, hid = sb("act_s", [P, 2, HID]), sb("hid", [P, 2, HP])
        hT = sb("hT", [P, 2, HP])
        yo = sb("yo", [P, 2, D])

        bank = [ctx.enter_context(nc.psum_tensor(f"bank{i}", [P, 512], f32)) for i in range(8)]

        s_in = sem("s_in")
        warm_zero = sem("warm_zero")
        s_xres = sem("s_xres")
        s_moew = sem("s_moew")
        s_zero = sem("s_zero")
        s_blank = sem("s_blank")
        s_xT = sem("s_xT")
        xt_done = sem("xt_done")
        qkv_done = sem("qkv_done")
        proj_done = sem("proj_done")
        projev_done = sem("projev_done")
        kd_done = sem("kd_done")
        scores_done = sem("scores_done")
        att_done = sem("att_done")
        u_done = sem("u_done")
        um_done = sem("um_done")
        st_done = sem("st_done")
        y_done = sem("y_done")
        yev_done = sem("yev_done")
        yst_done = sem("yst_done")
        dch = sem("dch")
        gnst = sem("gnst")
        gnpe = sem("gnpe")
        var_ready = sem("var_ready")
        rstd_done = sem("rstd_done")
        gnab_done = sem("gnab_done")
        yn_done = sem("yn_done")
        o_done = sem("o_done")
        z_done = sem("z_done")
        x1_done = sem("x1_done")
        x1t_pe = sem("x1t_pe")
        x1t_done = sem("x1t_done")
        logit_done = sem("logit_done")
        d_done = sem("d_done")
        exp_done = sem("exp_done")
        oh_done = sem("oh_done")
        rank_done = sem("rank_done")
        prob_done = sem("prob_done")
        rank_read = sem("rank_read")
        slot_done = sem("slot_done")
        table_done = sem("table_done")
        xs_done = sem("xs_done")
        scat_done = [sem(f"scat_done{b}") for b in range(B)]
        xg_loaded = [sem("xg_loaded0"), sem("xg_loaded1")]
        t1_done = sem("t1_done")
        xgT_done = sem("xgT_done")
        gate_done = sem("gate_done")
        up_done = sem("up_done")
        silu_done = sem("silu_done")
        hid_done = sem("hid_done")
        t2_done = sem("t2_done")
        hT_done = sem("hT_done")
        down_done = sem("down_done")
        yo_done = sem("yo_done")
        yo_stored = [sem("yo_stored0"), sem("yo_stored1")]
        gath_done = [[sem(f"gath_done{b}{h}") for h in range(2)] for b in range(B)]
        out_ready = sem("out_ready")
        stored = sem("stored")

        N_IN = 10 * 16
        HALF = PAIRS // 2
        spare = [(bank[4], bank[5]), (bank[7], bank[7])]

        block = ctx.enter_context(nc.Block())

        def bcast(ap, n):
            return ap.unsqueeze(2).broadcast_to([ap.shape[0], ap.shape[1], n])

        def vdiag(u):
            v = vx[:, u, :]
            step = v.ap[-1][0]
            return bass.AP(v.tensor, v.offset, [v.ap[0], [P * step, NG], [(32 + DH) * step, HG], [step, DH]])

        @block.sync
        def _(sp):
            for dst, src in ((wq_s, wqT), (wk_s, wkT), (wv_s, wvT)):
                sp.dma_start(dst[:, :], src).then_inc(s_in, 16)
            sp.dma_start(xt[:, :, :].rearrange("p n t -> p (n t)"), x_T[:, 0:2 * P]).then_inc(s_in, 16)
            sp.dma_start(cst[:, :], const).then_inc(s_in, 16)
            for dst, src in ((wo_s, woT), (gate_s, gateT), (eb_s, ebias)):
                sp.dma_start(dst[:, :], src).then_inc(s_in, 16)
            sp.dma_start(gn_s[:, 0:1], gnw).then_inc(s_in, 16)
            sp.dma_start(gn_s[:, 1:2], gnb).then_inc(s_in, 16)
            sp.dma_start(xT_all[:, :], x_T).then_inc(s_xT, 16)
            sp.dma_start(xres[:, :, :], x_tok.rearrange("(n p) d -> p n d", p=P)).then_inc(s_xres, 16)

            def load_tile(b, n, u, reuse=True):
                if reuse:
                    sp.wait_ge(t1_done, b * TILES + n - 1)
                sp.dma_start(xg[:, u, :], routed[b][bass.ds(n * P, P), :]).then_inc(xg_loaded[u], 16)

            def store_tile(b, n, u):
                sp.wait_ge(yo_done, b * TILES + n + 1)
                sp.dma_start(answers[b][bass.ds(n * P, P), :], yo[:, u, :]).then_inc(yo_stored[u], 16)

            LAG = TILES % 2 + 4
            for b in range(B):
                sp.wait_ge(scat_done[b], 16 * TOPK * PAIRS)
                u0 = b * TILES % 2
                for n in range(LAG):
                    load_tile(b, n, (u0 + n) % 2, b > 0 or n > 1)
                    if b:
                        store_tile(b - 1, TILES - LAG + n, (TILES - LAG + n) % 2)
                with sp.Fori(0, (TILES - LAG) // 2) as i:
                    for w in range(2):
                        load_tile(b, 2 * i + LAG + w, (u0 + LAG + w) % 2)
                        store_tile(b, 2 * i + w, (u0 + w) % 2)
            for n in range(TILES - LAG, TILES):
                store_tile(B - 1, n, (u0 + n) % 2)

            for b in range(B):
                for h in range(2):
                    sp.wait_ge(out_ready, 2 * b + h + 1)
                    t0 = b * PAIRS + h * HALF
                    sp.dma_start(out.rearrange("(n p) d -> p n d", p=P)[:, t0:t0 + HALF, :],
                                 z[:, t0:t0 + HALF, :]).then_inc(stored, 16)
            sp.wait_ge(stored, 16 * 2 * B)

        @block.gpsimd
        def _(pool):
            for n, a in enumerate((zeros[:, :], vx[:, :, :], hid[:, :, HID:HP], w_s[HID - (HC - 1) * P:P, :, WCOLS - D:WCOLS], cum[:, 0:1])):
                pool.memset(a, 0.0).then_inc(s_zero, 1)
                pool.wait_ge(s_zero, n + 1)
            pool.wait_ge(s_in, N_IN)

            def rstd(dst, src):
                pool.tensor_tensor(out=dst, in0=src, in1=const_of("half")[:, 0:dst.shape[1]], op=ALU.pow)\
                    .then_inc(rstd_done, 1)

            def scatter(b):
                for k in range(TOPK):
                    for n in range(PAIRS):
                        pool.wait_ge(xs_done, TOPK * PAIRS * b + k * PAIRS + n + 1)
                        pool.indirect_dma_start(
                            out=routed[b][:, :], out_offset=bass.IndirectOffsetOnAxis(ap=slot[:, b, k, n:n + 1], axis=0),
                            in_=xs[:, b, k, n, :], in_offset=None).then_inc(scat_done[b], 16)

            def gather(b, h):
                for n in range(h * HALF, (h + 1) * HALF):
                    for k in range(TOPK):
                        pool.indirect_dma_start(
                            out=xs[:, b, k, n, :], out_offset=None, in_=answers[b][:, :],
                            in_offset=bass.IndirectOffsetOnAxis(ap=slot[:, b, k, n:n + 1], axis=0))\
                            .then_inc(gath_done[b][h], 16)

            for b in range(B):
                pool.wait_ge(var_ready, 3 * b + 1)
                rstd(gn[:, 6:7], gn[:, 5:6])
                for h in range(2):
                    pool.wait_ge(var_ready, 3 * b + 2 + h)
                    rstd(lrstd[:, h * HALF:(h + 1) * HALF], lvar[:, h * HALF:(h + 1) * HALF])
                pool.wait_ge(slot_done, b + 1)
                if b == 0:
                    pool.wait_ge(s_blank, 16 * B)
                scatter(b)
            for b in range(B):
                last = (b + 1) * TILES
                pool.wait_ge(yo_stored[0], 16 * ((last + 1) // 2))
                pool.wait_ge(yo_stored[1], 16 * (last // 2))
                pool.wait_ge(scat_done[b], 16 * TOPK * PAIRS)
                for h in range(2):
                    gather(b, h)
                for h in range(2):
                    pool.wait_ge(var_ready, 3 * B + 2 * b + h + 1)
                    rstd(lrstd[:, h * HALF:(h + 1) * HALF], lvar[:, h * HALF:(h + 1) * HALF])

        @block.scalar
        def _(act):
            act.wait_ge(s_in, N_IN)

            def evacuate(p, u, reuse=True):
                act.wait_ge(qkv_done, p + 1)
                if reuse:
                    act.wait_ge(y_done, p - 1)
                nc.scalar.copy(qT[:, u, :], bank[0][:, 0:P])
                nc.scalar.copy(kT[:, u, :], bank[0][:, P:2 * P])
                nc.scalar.copy(vdiag(u), bank[0][:, 2 * P:3 * P].rearrange("p (g i d) -> p g i d", g=NG, i=HG))
                for i in range(HG):
                    last = nc.scalar.activation(qx[:, u, i, :], bank[0][:, 0:P], ACT.Copy, scale=headsel[:, i:i + 1])
                last.then_inc(projev_done, 1)

            def next_pair(p, u):
                act.wait_ge(proj_done, p + 1)
                nc.scalar.copy(xt[:, u, :], xT_all[:, bass.ds((p + 2) * P, P)]).then_inc(xt_done, 1)

            def load_expert_weights():
                for b in range(B):
                    act.dma_start(routed[b].rearrange("(n p) d -> p n d", p=P),
                                  zeros[:, :].unsqueeze(1).broadcast_to([P, TILES, D])).then_inc(s_blank, 16)
                act.dma_start(w_s[:, :, 0:HID], w1.rearrange("e p n -> p e n")).then_inc(s_moew, 16)
                act.dma_start(w_s[:, :, HID:2 * HID], w3.rearrange("e p n -> p e n")).then_inc(s_moew, 16)
                for c in range(HC):
                    rows = min(P, HID - c * P)
                    act.dma_start(w_s[0:rows, :, 2 * HID + c * D:2 * HID + (c + 1) * D], w2[:, c * P:c * P + rows, :].rearrange("e p n -> p e n"))\
                        .then_inc(s_moew, 16)

            def norm_y(b):
                act.wait_ge(gnab_done, b + 1)
                if b > 0:
                    act.wait_ge(o_done, 2 * b)
                for h in range(2):
                    t0 = b * T + h * HALF * P
                    nc.scalar.activation(yn[:, h * HALF * P:(h + 1) * HALF * P], yT[:, t0:t0 + HALF * P], ACT.Identity,
                                         scale=gn[:, 7:8], bias=gn[:, 9:10]).then_inc(yn_done, 1)

            def x1_T(b, h):
                act.wait_ge(x1t_pe, 2 * b + h + 1)
                if b > 0 and h == 0:
                    act.wait_ge(logit_done, b)
                nc.scalar.copy(x1T[:, h * HALF:(h + 1) * HALF, :],
                               spare[b][h][:, :].rearrange("p (n d) -> p n d", n=HALF)).then_inc(x1t_done, 1)

            def exp_logits(b):
                act.wait_ge(d_done, b + 1)
                nc.scalar.activation(rt["ex"][:, :, :], rt["d"][:, :, :], ACT.Exp).then_inc(exp_done, 1)

            def weigh_rows(b, k, h):
                act.wait_ge(prob_done, b + 1)
                for n in range(h * HALF, (h + 1) * HALF):
                    nc.scalar.activation(xs[:, b, k, n, :], x1[:, b * PAIRS + n, :], ACT.Copy,
                                         scale=prob[:, k, n:n + 1]).then_inc(xs_done, 1)

            act.wait_ge(s_zero, 5)
            evacuate(0, 0, False)
            act.wait_ge(s_xT, 16)
            next_pair(0, 0)
            evacuate(1, 1, False)
            next_pair(1, 1)
            load_expert_weights()
            with act.Fori(0, PAIRS // 2 - 1) as i:
                for u in range(2):
                    evacuate(2 + 2 * i + u, u)
                    next_pair(2 + 2 * i + u, u)
            for n in range(PAIRS):
                evacuate(PAIRS + n, n % 2)
                if n == 0:
                    norm_y(0)
                if n < PAIRS - 2:
                    next_pair(PAIRS + n, n % 2)
                if n == 2:
                    x1_T(0, 0)
                elif n == 3:
                    x1_T(0, 1)
                    exp_logits(0)
                elif n in (5, 6):
                    weigh_rows(0, n - 5, 0)
                    weigh_rows(0, n - 5, 1)
            norm_y(1)

            def silu(g, u, reuse=True):
                act.wait_ge(gate_done, g + 1)
                if reuse:
                    act.wait_ge(hid_done, g - 1)
                nc.scalar.activation(act_s[:, u, :], bank[1 + u][:, 0:HID], ACT.Silu).then_inc(silu_done, 1)

            def hidden_T(g, u, reuse=True):
                act.wait_ge(t2_done, g + 1)
                if reuse:
                    act.wait_ge(down_done, g - 1)
                nc.scalar.copy(hT[:, u, :], bank[5][:, 0:HP]).then_inc(hT_done, 1)

            def tile_step(g, u):
                silu(g, u)
                hidden_T(g - 1, 1 - u)

            silu(0, 0, False)
            silu(1, 1, False)
            hidden_T(0, 0, False)
            silu(2, 0)
            hidden_T(1, 1, False)
            for g in range(3, ROUTED):
                tile_step(g, g % 2)
                if g == 5:
                    x1_T(1, 0)
                elif g == 6:
                    x1_T(1, 1)
                elif g == 7:
                    exp_logits(1)
                elif g in (10, 11, 12, 13):
                    weigh_rows(1, (g - 10) // 2, g % 2)
            with act.Fori(0, (NT - ROUTED) // 2) as i:
                for u in range(2):
                    tile_step(2 * i + ROUTED + u, u)
            hidden_T(NT - 1, 1)

        @block.vector
        def _(dve):
            chain = [0]

            def link(ins):
                chain[0] += 1
                ins.then_inc(dch, 1)
                dve.wait_ge(dch, chain[0])

            V = nc.vector

            def decay_k(p, u):
                dve.wait_ge(proj_done, p + 1)
                V.tensor_tensor(out=kd[:, u, :, :], in0=bank[1][:, 0:D].unsqueeze(1).broadcast_to([P, 2, D]),
                                in1=kdecay, op=ALU.mult).then_inc(kd_done, 1)

            def decay_scores(p, u):
                for half in range(2):
                    dve.wait_ge(scores_done, 2 * p + half + 1)
                    for g in (2 * half, 2 * half + 1):
                        ins = V.tensor_tensor(out=att[:, u, g, :], in0=bank[2 + g][:, 0:HG * C],
                                              in1=causal[:, g, :], op=ALU.mult)
                    ins.then_inc(att_done, 1)

            def states(p, u):
                dve.wait_ge(u_done, p + 1)
                V.tensor_tensor(out=um[:, :, :], in0=bank[1][:, P:3 * P].rearrange("p (j n) -> p j n", j=2),
                                in1=blockdiag.unsqueeze(1).broadcast_to([P, 2, D]), op=ALU.mult).then_inc(um_done, 1)
                dve.wait_ge(um_done, p + 1)
                dve.wait_ge(y_done, p)
                V.scalar_tensor_tensor(out=s1[:, u, :], in0=s0[:, u, :], scalar=sdecay[:, 0:1], in1=um[:, 0, :],
                                       op0=ALU.mult, op1=ALU.add)
                V.scalar_tensor_tensor(out=s0[:, 1 - u, :], in0=s0[:, u, :], scalar=sdecay[:, 1:2], in1=um[:, 1, :],
                                       op0=ALU.mult, op1=ALU.add).then_inc(st_done, 1)
                dve.wait_ge(st_done, p + 1)

            def evacuate_y(p):
                dve.wait_ge(y_done, p + 1)
                for j in range(2):
                    ins = V.tensor_tensor(out=yT[:, bass.ds(p * P + j * C, C)], in0=bank[6 + j][:, 0:C], in1=ydecay,
                                          op=ALU.mult)
                ins.then_inc(yev_done, 1)
                dve.wait_ge(yev_done, p + 1)
                V.bn_stats(out=ystats[:, :, :].rearrange("p n s -> p (n s)")[:, bass.ds(p * 6, 6)],
                           in_=yT[:, bass.ds(p * P, P)]).then_inc(yst_done, 1)

            def norm_stats(b, h):
                halves = range(h * HALF, (h + 1) * HALF)
                for n in halves:
                    ins = V.bn_stats(out=lstats[:, n, :], in_=z[:, b * PAIRS + n, :])
                link(ins)
                for n in halves:
                    ins = V.bn_aggr(out=lmv[:, n, :], in_=lstats[:, n, :])
                link(ins)
                V.tensor_scalar(lvar[:, halves[0]:halves[-1] + 1], lmv[:, halves[0]:halves[-1] + 1, 1], EPS, None, ALU.add)\
                    .then_inc(var_ready, 1)

            def norm_apply(b, h, dst, n_var, done):
                dve.wait_ge(rstd_done, n_var)
                for n in range(h * HALF, (h + 1) * HALF):
                    ins = V.tensor_scalar(dst[:, b * PAIRS + n, :], z[:, b * PAIRS + n, :], lmv[:, n, 0:1],
                                          lrstd[:, n:n + 1], ALU.subtract, ALU.mult)
                ins.then_inc(done, 1)

            def group_norm(b):
                dve.wait_ge(yst_done, (b + 1) * PAIRS)
                V.bn_aggr(out=gn[:, 0:2], in_=ystats[:, b * PAIRS:(b + 1) * PAIRS, :].rearrange("p n s -> p (n s)"))\
                    .then_inc(gnst, 1)
                sums = spare[b][1]
                dve.wait_ge(gnpe, 2 * b + 1)
                link(V.tensor_copy(gn[:, 2:4], sums[:, 0:2]))
                link(V.tensor_tensor(out=gn[:, 11:12], in0=gn[:, 0:1], in1=gn[:, 2:3], op=ALU.subtract))
                V.tensor_tensor(out=gn[:, 4:5], in0=gn[:, 11:12], in1=gn[:, 11:12], op=ALU.mult).then_inc(gnst, 1)
                dve.wait_ge(gnpe, 2 * b + 2)
                V.scalar_tensor_tensor(out=gn[:, 5:6], in0=sums[:, 2:3], scalar=EPS, in1=gn[:, 3:4],
                                       op0=ALU.add, op1=ALU.add).then_inc(var_ready, 1)
                dve.wait_ge(rstd_done, 3 * b + 1)
                link(V.tensor_tensor(out=gn[:, 7:8], in0=gn[:, 6:7], in1=gn_s[:, 0:1], op=ALU.mult))
                link(V.tensor_tensor(out=gn[:, 8:9], in0=gn[:, 2:3], in1=gn[:, 7:8], op=ALU.mult))
                V.tensor_tensor(out=gn[:, 9:10], in0=gn_s[:, 1:2], in1=gn[:, 8:9], op=ALU.subtract).then_inc(gnab_done, 1)

            def residual(b, h):
                dve.wait_ge(o_done, 2 * b + h + 1)
                t0 = b * PAIRS + h * HALF
                V.tensor_tensor(out=z[:, t0:t0 + HALF, :], in0=spare[b][h][:, :].rearrange("p (n d) -> p n d", n=HALF),
                                in1=xres[:, t0:t0 + HALF, :], op=ALU.add).then_inc(z_done, 1)

            t3 = {n: a[:, :, :] for n, a in rt.items()}
            desc = const_of("rank_e").rearrange("p (n e) -> p n e", e=NE)
            n64 = NE * PAIRS

            def read_logits(b):
                logits = spare[b][0][:, 0:n64].rearrange("p (n e) -> p n e", e=NE)
                dve.wait_ge(logit_done, b + 1)
                link(V.tensor_reduce(r8["mx"][:, :], logits, AX, ALU.max))
                V.tensor_tensor(out=t3["d"], in0=logits, in1=bcast(r8["mx"][:, :], NE), op=ALU.subtract).then_inc(d_done, 1)

            def softmax(b):
                dve.wait_ge(exp_done, b + 1)
                link(V.tensor_reduce(r8["sum"][:, :], t3["ex"], AX, ALU.add))
                link(V.reciprocal(r8["rc"][:, :], r8["sum"][:, :]))
                link(V.tensor_tensor(out=t3["sc"], in0=t3["ex"], in1=bcast(r8["rc"][:, :], NE), op=ALU.mult))
                link(V.tensor_tensor(out=t3["key"], in0=t3["sc"],
                                     in1=eb_s[:, :].unsqueeze(1).broadcast_to([P, PAIRS, NE]), op=ALU.add))

            def choose(k):
                oh = t3[f"oh{k + 1}"]
                link(V.tensor_reduce(r8["m"][:, :], t3["key"], AX, ALU.max))
                link(V.tensor_tensor(out=t3["eq"], in0=t3["key"], in1=bcast(r8["m"][:, :], NE), op=ALU.is_equal))
                link(V.tensor_tensor(out=t3["w"], in0=t3["eq"], in1=desc, op=ALU.mult))
                link(V.tensor_reduce(r8["f"][:, :], t3["w"], AX, ALU.max))
                link(V.tensor_tensor(out=oh, in0=desc, in1=bcast(r8["f"][:, :], NE), op=ALU.is_equal))
                if k == 0:
                    link(V.scalar_tensor_tensor(out=t3["key"], in0=oh, scalar=-3e38, in1=t3["key"],
                                                op0=ALU.mult, op1=ALU.add))
                else:
                    V.tensor_tensor(out=ohe[:, :, :].rearrange("p e n -> p n e"), in0=t3["oh1"], in1=t3["oh2"],
                                    op=ALU.add).then_inc(oh_done, 1)

            def chosen_scores():
                for k in range(TOPK):
                    link(V.tensor_tensor(out=t3["w"], in0=t3["sc"], in1=t3[f"oh{k + 1}"], op=ALU.mult))
                    ins = V.tensor_reduce(prob[:, k, :], t3["w"], AX, ALU.add)
                    if k == 0:
                        link(ins)
                ins.then_inc(prob_done, 1)

            within, counts = rank[:, 0:n64], rank[:, n64:2 * n64]
            flat_pos = pos[:, :, :].rearrange("p e n -> p (e n)")

            def read_ranks(b):
                dve.wait_ge(rank_done, b + 1)
                V.tensor_copy(rank[:, :], spare[b][1][:, 0:2 * n64]).then_inc(rank_read, 1)
                dve.wait_ge(rank_read, b + 1)

            def expert_starts():
                link(V.tensor_tensor_scan(cum[:, 1:n64 + 1], const_of("ones")[:, 0:n64], counts, 0.0, ALU.mult, ALU.add))
                link(V.tensor_tensor(out=flat_pos, in0=cum[:, 1:n64 + 1], in1=counts, op=ALU.subtract))
                starts, ends = cum[:, 0:n64:PAIRS], cum[:, PAIRS:n64 + 1:PAIRS]
                link(V.tensor_tensor(out=r8["tot"][:, :], in0=ends, in1=starts, op=ALU.subtract))
                link(V.tensor_tensor(out=gtt[:, :, :], in0=bcast(r8["tot"][:, :], NE),
                                     in1=const_of("tilestart").rearrange("p (e j) -> p e j", j=NE), op=ALU.is_gt))
                link(V.tensor_reduce(r8["nt"][:, :], gtt[:, :, :], AX, ALU.add))
                link(V.tensor_tensor_scan(r8["te"][:, :], const_of("ones")[:, 0:NE], r8["nt"][:, :], 0.0, ALU.mult, ALU.add))
                link(V.tensor_tensor(out=r8["ts"][:, :], in0=r8["te"][:, :], in1=r8["nt"][:, :], op=ALU.subtract))
                link(V.scalar_tensor_tensor(out=r8["off"][:, :], in0=r8["ts"][:, :], scalar=float(P), in1=starts,
                                            op0=ALU.mult, op1=ALU.subtract))

            def slots(b):
                link(V.tensor_tensor(out=pos[:, :, :], in0=pos[:, :, :], in1=bcast(r8["off"][:, :], PAIRS), op=ALU.add))
                link(V.tensor_tensor(out=flat_pos, in0=flat_pos, in1=within, op=ALU.add))
                for k in range(TOPK):
                    link(V.tensor_tensor(out=t3["w"], in0=t3[f"oh{k + 1}"], in1=pos[:, :, :].rearrange("p e n -> p n e"),
                                         op=ALU.mult))
                    link(V.tensor_reduce(r8["sl"][:, :], t3["w"], AX, ALU.add))
                    ins = V.tensor_copy(slot[:, b, k, :], r8["sl"][:, :])
                    if k == 0:
                        link(ins)
                ins.then_inc(slot_done, 1)

            def expert_table(b):
                link(V.tensor_tensor(out=tcmp[:, :, :], in0=const_of("tileid", 1).rearrange("p (g e) -> p g e", e=NE),
                                     in1=r8["te"][0:1, :].unsqueeze(1).broadcast_to([1, TILES, NE]), op=ALU.is_ge))
                link(V.tensor_reduce(tsum[:, :], tcmp[:, :, :], AX, ALU.add))
                V.tensor_scalar(expert[:, b * TILES:(b + 1) * TILES], tsum[:, :], float(NE - 1), float(WCOLS),
                                ALU.min, ALU.mult).then_inc(table_done, 1)

            def pair_step(p, u):
                evacuate_y(p - 1)
                decay_scores(p, u)
                states(p, u)
                decay_k(p + 1, 1 - u)

            V.memset(warm[:, :], 0.0).then_inc(warm_zero, 1)
            dve.wait_ge(s_in, N_IN)
            dve.wait_ge(s_zero, 5)
            link(V.memset(s0[:, 0, :], 0.0))
            decay_k(0, 0)
            decay_scores(0, 0)
            states(0, 0)
            decay_k(1, 1)
            with dve.Fori(0, PAIRS // 2 - 1) as i:
                for w in range(2):
                    pair_step(2 * i + 1 + w, (1 + w) % 2)
            evacuate_y(PAIRS - 2)
            decay_scores(PAIRS - 1, 1)
            states(PAIRS - 1, 1)
            evacuate_y(PAIRS - 1)
            group_norm(0)
            p1 = PAIRS
            link(V.memset(s0[:, 0, :], 0.0))
            decay_k(p1, 0)
            decay_scores(p1, 0)
            states(p1, 0)
            decay_k(p1 + 1, 1)
            dve.wait_ge(s_xres, 16)
            residual(0, 0)
            residual(0, 1)
            dve.wait_ge(z_done, 1)
            norm_stats(0, 0)
            pair_step(p1 + 1, 1)
            norm_apply(0, 0, x1, 2, x1_done)
            dve.wait_ge(z_done, 2)
            norm_stats(0, 1)
            pair_step(p1 + 2, 0)
            norm_apply(0, 1, x1, 3, x1_done)
            read_logits(0)
            softmax(0)
            pair_step(p1 + 3, 1)
            choose(0)
            choose(1)
            chosen_scores()
            read_ranks(0)
            pair_step(p1 + 4, 0)
            expert_starts()
            slots(0)
            pair_step(p1 + 5, 1)
            expert_table(0)
            pair_step(p1 + 6, 0)
            evacuate_y(p1 + 6)
            decay_scores(p1 + 7, 1)
            states(p1 + 7, 1)
            evacuate_y(p1 + 7)
            group_norm(1)

            def rows_T(g, u):
                dve.wait_ge(t1_done, g + 1)
                V.tensor_copy(xgT[:, u, :], bank[0][:, 0:P]).then_inc(xgT_done, 1)

            def hidden(g, u, reuse=True):
                dve.wait_ge(silu_done, g + 1)
                dve.wait_ge(up_done, g + 1)
                if reuse:
                    dve.wait_ge(t2_done, g - 1)
                V.tensor_tensor(out=hid[:, u, 0:HID], in0=bank[3 + u][:, 0:HID], in1=act_s[:, u, :], op=ALU.mult)\
                    .then_inc(hid_done, 1)

            def answer(g, u, slot_wait):
                dve.wait_ge(down_done, g + 1)
                if slot_wait is not None:
                    dve.wait_ge(yo_stored[u], slot_wait)
                V.tensor_copy(yo[:, u, :], bank[6][:, 0:D]).then_inc(yo_done, 1)

            def combine(b, h):
                dve.wait_ge(gath_done[b][h], 16 * TOPK * HALF)
                n = slice(h * HALF, (h + 1) * HALF)
                t = slice(b * PAIRS + h * HALF, b * PAIRS + (h + 1) * HALF)
                link(V.tensor_tensor(out=z[:, t, :], in0=xs[:, b, 0, n, :], in1=xs[:, b, 1, n, :], op=ALU.add))
                link(V.tensor_tensor(out=z[:, t, :], in0=z[:, t, :], in1=x1[:, t, :], op=ALU.add))
                norm_stats(b, h)

            def tile_step(g, half, u):
                hidden(g, u)
                answer(g - 2, u, 16 * (half - 1))
                rows_T(g + 2, u)

            def tile_steps(lo, hi):
                with dve.Fori(0, (hi - lo) // 2) as i:
                    for u in range(2):
                        tile_step(2 * i + lo + u, i + lo // 2, u)

            rows_T(0, 0)
            rows_T(1, 1)
            hidden(0, 0, False)
            rows_T(2, 0)
            hidden(1, 1, False)
            rows_T(3, 1)
            residual(1, 0)
            hidden(2, 0)
            answer(0, 0, None)
            rows_T(4, 0)
            dve.wait_ge(z_done, 3)
            norm_stats(1, 0)
            residual(1, 1)
            hidden(3, 1)
            answer(1, 1, None)
            rows_T(5, 1)
            dve.wait_ge(z_done, 4)
            norm_stats(1, 1)
            for g in range(4, ROUTED):
                tile_step(g, g // 2, g % 2)
                if g == 4:
                    norm_apply(1, 0, x1, 5, x1_done)
                elif g == 5:
                    norm_apply(1, 1, x1, 6, x1_done)
                elif g == 7:
                    read_logits(1)
                elif g == 8:
                    softmax(1)
                    choose(0)
                elif g == 9:
                    choose(1)
                elif g == 10:
                    chosen_scores()
                    read_ranks(1)
                elif g == 11:
                    expert_starts()
                elif g == 12:
                    slots(1)
                elif g == 13:
                    expert_table(1)
            tile_steps(ROUTED, COMBINED)
            combine(0, 0)
            tile_step(COMBINED, COMBINED // 2, 0)
            combine(0, 1)
            tile_step(COMBINED + 1, COMBINED // 2, 1)
            norm_apply(0, 0, z, 3 * B + 1, out_ready)
            tile_step(COMBINED + 2, COMBINED // 2 + 1, 0)
            norm_apply(0, 1, z, 3 * B + 2, out_ready)
            tile_step(COMBINED + 3, COMBINED // 2 + 1, 1)
            tile_steps(COMBINED + 4, NT - 2)
            hidden(NT - 2, 0)
            answer(NT - 4, 0, 16 * (NT // 2 - 2))
            hidden(NT - 1, 1)
            answer(NT - 3, 1, 16 * (NT // 2 - 2))
            answer(NT - 2, 0, 16 * (NT // 2 - 1))
            answer(NT - 1, 1, 16 * (NT // 2 - 1))
            for h in range(2):
                combine(B - 1, h)
            for h in range(2):
                norm_apply(B - 1, h, z, 3 * B + 2 + h + 1, out_ready)

        @block.tensor
        def _(pe):
            MM = nc.tensor.matmul

            def keep_warm(rounds):
                with pe.Fori(0, rounds):
                    for _ in range(4):
                        MM(bank[7][:, :], warm[:, 0:P], warm[:, :], start=True, stop=True)

            def fill(dst, n):
                for _ in range(n):
                    MM(dst, warm[:, 0:P], warm[:, 0:dst.shape[1]], start=True, stop=True)

            idle = slice(HG * C, 2 * HG * C)
            pe.wait_ge(warm_zero, 1)
            keep_warm(13)
            pe.wait_ge(s_in, N_IN)
            pe.wait_ge(s_zero, 5)

            def project(p, u, p_loaded=True):
                x = xt[:, u, :]
                if p_loaded:
                    pe.wait_ge(xt_done, p - 1)
                pe.wait_ge(projev_done, p)
                fill(bank[0][:, 3 * P:4 * P], 2)
                MM(bank[0][:, 0:P], wq_s[:, :], x, start=True, stop=True)
                MM(bank[0][:, P:2 * P], wk_s[:, :], x, start=True, stop=True)
                MM(bank[0][:, 2 * P:3 * P], x, wv_s[:, :], start=True, stop=True).then_inc(qkv_done, 1)
                pe.wait_ge(um_done, p)
                MM(bank[1][:, 0:D], x, wk_s[:, :], start=True, stop=True).then_inc(proj_done, 1)

            def scores(p, u, spare_read=None):
                pe.wait_ge(projev_done, p + 1)
                if spare_read is not None:
                    fill(bank[2][:, idle], 12)
                for half in range(2):
                    if half and spare_read is not None:
                        pe.wait_ge(*spare_read)
                    for j, gg in ((0, 0), (1, 1), (1, 0), (0, 1)):
                        g = 2 * half + gg
                        if gg == j:
                            fill(bank[2 + g][:, idle], 1)
                        r = slice(32 * g, 32 * g + 32)
                        c = slice(C * j, C * j + C)
                        last = MM(bank[2 + g][c, 0:HG * C], kT[r, u, c], qx[r, u, :, c], start=True, stop=True)
                    last.then_inc(scores_done, 1)

            def increments(p, u):
                pe.wait_ge(kd_done, p + 1)
                for j in range(2):
                    last = MM(bank[1][:, (1 + j) * P:(2 + j) * P], kd[:, u, j, :], vdiag(u), start=True, stop=True)
                last.then_inc(u_done, 1)

            def outputs(p, u):
                pe.wait_ge(att_done, 2 * p + 2)
                pe.wait_ge(yev_done, p)
                for i in range(HG):
                    fill(bank[2][:, idle], 1)
                    for g in range(NG):
                        for j in range(2):
                            c = slice(C * j, C * j + C)
                            h = g * HG + i
                            MM(bank[6 + j][32 * g:32 * g + 32, 0:C], vx[c, u, 32 * h:32 * h + 32],
                               att[c, u, g, i * C:(i + 1) * C], start=i == 0, stop=False, skip_group_check=True)
                pe.wait_ge(st_done, p + 1)
                for j, s in enumerate((s0, s1)):
                    last = MM(bank[6 + j][:, 0:C], s[:, u, :], qT[:, u, C * j:C * j + C], start=False, stop=True,
                              skip_group_check=True)
                last.then_inc(y_done, 1)

            def pair_step(p, u, spare_read=None):
                scores(p, u, spare_read)
                increments(p, u)
                project(p + 1, 1 - u)
                outputs(p, u)

            def head_means(b):
                sums = spare[b][1]
                fill(bank[2][:, idle], 8)
                pe.wait_ge(gnst, 2 * b + 1)
                MM(sums[:, 0:2], headmean, gn[:, 0:2], start=True, stop=True).then_inc(gnpe, 1)
                fill(bank[2][:, idle], 6)
                pe.wait_ge(gnst, 2 * b + 2)
                MM(sums[:, 2:3], headmean, gn[:, 4:5], start=True, stop=True).then_inc(gnpe, 1)

            def project_y(b, h):
                pe.wait_ge(yn_done, 2 * b + h + 1)
                if spare[b][0] is spare[b][1] and h:
                    pe.wait_ge(z_done, 2 * b + 1)
                for n in range(HALF):
                    t0 = (h * HALF + n) * P
                    last = MM(spare[b][h][:, n * D:(n + 1) * D], yn[:, t0:t0 + P], wo_s[:, :], start=True, stop=True)
                last.then_inc(o_done, 1)

            def transpose_x1(b, h):
                pe.wait_ge(x1_done, 2 * b + h + 1)
                if spare[b][0] is spare[b][1] and h:
                    pe.wait_ge(x1t_done, 2 * b + 1)
                for n in range(h * HALF, (h + 1) * HALF):
                    last = nc.tensor.transpose(spare[b][h][:, (n % HALF) * P:(n % HALF + 1) * P],
                                               x1[:, b * PAIRS + n, :], ident)
                last.then_inc(x1t_pe, 1)

            def router_logits(b):
                for n in range(PAIRS):
                    if n == 0:
                        pe.wait_ge(x1t_done, 2 * b + (1 if spare[b][0] is not spare[b][1] else 2))
                    elif n == HALF:
                        pe.wait_ge(x1t_done, 2 * b + 2)
                    last = MM(spare[b][0][:, n * NE:(n + 1) * NE], x1T[:, n, :], gate_s[:, :], start=True, stop=True)
                last.then_inc(logit_done, 1)

            def ranks(b):
                pe.wait_ge(oh_done, b + 1)
                n64 = NE * PAIRS
                o = ohe[:, :, :].rearrange("p e n -> p (e n)")
                MM(spare[b][1][:, 0:n64], const_of("before"), o, start=True, stop=True)
                MM(spare[b][1][:, n64:2 * n64], const_of("ones"), o, start=True, stop=True).then_inc(rank_done, 1)

            project(0, 0, False)
            scores(0, 0)
            increments(0, 0)
            project(1, 1, False)
            outputs(0, 0)
            with pe.Fori(0, PAIRS // 2 - 1) as i:
                for w in range(2):
                    pair_step(2 * i + 1 + w, (1 + w) % 2)
            scores(PAIRS - 1, 1)
            increments(PAIRS - 1, 1)
            outputs(PAIRS - 1, 1)
            p1 = PAIRS
            project(p1, 0)
            head_means(0)
            scores(p1, 0, (var_ready, 1))
            increments(p1, 0)
            project(p1 + 1, 1)
            outputs(p1, 0)
            project_y(0, 0)
            project_y(0, 1)
            pair_step(p1 + 1, 1, (z_done, 2))
            transpose_x1(0, 0)
            pair_step(p1 + 2, 0, (x1t_done, 1))
            transpose_x1(0, 1)
            router_logits(0)
            pair_step(p1 + 3, 1, (d_done, 1))
            ranks(0)
            pair_step(p1 + 4, 0, (rank_read, 1))
            pair_step(p1 + 5, 1)
            pair_step(p1 + 6, 0)
            scores(p1 + 7, 1)
            increments(p1 + 7, 1)
            outputs(p1 + 7, 1)
            head_means(1)

            next_up = [pe.alloc_register(f"next_up{u}") for u in range(2)]
            next_down = [pe.alloc_register(f"next_down{u}") for u in range(2)]

            def load_expert(g, u):
                pe.reg_load(next_up[u], expert[0:1, bass.ds(g, 1)])

            def transpose_rows(g, u, n_loaded):
                pe.wait_ge(xg_loaded[u], n_loaded)
                pe.wait_ge(xgT_done, g)
                nc.tensor.transpose(bank[0][:, 0:P], xg[:, u, :], ident).then_inc(t1_done, 1)

            w_flat = w_s[:, :, :].rearrange("p e n -> p (e n)")

            def gate_up(g, u):
                at = pe.snap(next_up[u], min_val=0, max_val=(NE - 1) * WCOLS)
                MM(bank[1 + u][:, 0:HID], xgT[:, u, :], w_flat[:, bass.ds(at, HID)], start=True, stop=True)\
                    .then_inc(gate_done, 1)
                MM(bank[3 + u][:, 0:HID], xgT[:, u, :], w_flat[:, bass.ds(at + HID, HID)], start=True, stop=True)\
                    .then_inc(up_done, 1)

            def transpose_hidden(g, u):
                pe.wait_ge(hid_done, g + 1)
                for c in range(HC):
                    last = nc.tensor.transpose(bank[5][:, c * P:(c + 1) * P], hid[:, u, c * P:(c + 1) * P], ident)
                last.then_inc(t2_done, 1)

            def down(g, u):
                at = pe.snap(next_down[u], min_val=0, max_val=(NE - 1) * WCOLS)
                pe.wait_ge(hT_done, g + 1)
                for c in range(HC):
                    last = MM(bank[6][:, 0:D], hT[:, u, c * P:(c + 1) * P], w_flat[:, bass.ds(at + (2 * HID + c * D), D)],
                              start=c == 0, stop=c == HC - 1)
                last.then_inc(down_done, 1)

            def advance(g, u, load=True):
                pe.reg_mov(next_down[u], next_up[u])
                if load:
                    load_expert(g + 2, u)

            def tile_step(g, half, u):
                gate_up(g, u)
                transpose_rows(g + 2, u, 16 * (half + 2))
                down(g - 2, u)
                advance(g, u)
                transpose_hidden(g - 1, 1 - u)

            def tile_steps(lo, hi):
                with pe.Fori(0, (hi - lo) // 2) as i:
                    for u in range(2):
                        tile_step(2 * i + lo + u, i + lo // 2, u)

            pe.wait_ge(s_moew, 16 * (2 + HC))
            pe.wait_ge(table_done, 1)
            load_expert(0, 0)
            load_expert(1, 1)
            transpose_rows(0, 0, 16)
            transpose_rows(1, 1, 16)
            gate_up(0, 0)
            transpose_rows(2, 0, 32)
            advance(0, 0)
            gate_up(1, 1)
            transpose_rows(3, 1, 32)
            advance(1, 1)
            project_y(1, 0)
            transpose_hidden(0, 0)
            for g in range(2, ROUTED):
                tile_step(g, g // 2, g % 2)
                if g == 2:
                    project_y(1, 1)
                elif g == 5:
                    transpose_x1(1, 0)
                elif g == 6:
                    transpose_x1(1, 1)
                elif g == 7:
                    router_logits(1)
                elif g == 10:
                    ranks(1)
            tile_steps(ROUTED, TILES - 3)
            pe.wait_ge(table_done, 2)
            tile_steps(TILES - 3, NT - 2)
            gate_up(NT - 2, 0)
            pe.wait_ge(xgT_done, NT)
            down(NT - 4, 0)
            advance(NT - 2, 0, False)
            transpose_hidden(NT - 3, 1)
            gate_up(NT - 1, 1)
            pe.wait_ge(yo_done, NT - 3)
            down(NT - 3, 1)
            advance(NT - 1, 1, False)
            transpose_hidden(NT - 2, 0)
            pe.wait_ge(yo_done, NT - 2)
            down(NT - 2, 0)
            transpose_hidden(NT - 1, 1)
            pe.wait_ge(yo_done, NT - 1)
            down(NT - 1, 1)


def kernel(L0_attn_x, L0_attn_W_q, L0_attn_W_k, L0_attn_W_v, L0_attn_W_o, L0_attn_gn_weight, L0_attn_gn_bias,
           L0_ffn_gate_w, L0_ffn_expert_bias, L0_ffn_w1, L0_ffn_w2, L0_ffn_w3):
    import concourse.bacc as bacc
    from concourse.bass_utils import run_bass_kernel_spmd

    def lay(a):
        return np.ascontiguousarray(a)

    x = np.asarray(L0_attn_x).reshape(B * T, D)
    arrays = {
        "x_tok": lay(x), "x_T": lay(x.T),
        "wqT": lay(np.asarray(L0_attn_W_q).T), "wkT": lay(np.asarray(L0_attn_W_k).T),
        "wvT": lay(np.asarray(L0_attn_W_v).T), "woT": lay(np.asarray(L0_attn_W_o).T),
        "gnw": lay(np.asarray(L0_attn_gn_weight).reshape(D, 1)), "gnb": lay(np.asarray(L0_attn_gn_bias).reshape(D, 1)),
        "gateT": lay(np.asarray(L0_ffn_gate_w).T),
        "ebias": lay(np.broadcast_to(np.asarray(L0_ffn_expert_bias)[None, :], (P, NE))),
        "w1": lay(L0_ffn_w1), "w2": lay(L0_ffn_w2), "w3": lay(L0_ffn_w3),
        "const": shape_constants(),
    }
    nc = bacc.Bacc("TRN2", target_bir_lowering=False, num_devices=1)
    args = [nc.dram_tensor(f"in_{n}", a.shape, mybir.dt.from_np(a.dtype), kind="ExternalInput").ap()
            for n, a in arrays.items()]
    args.append(nc.dram_tensor("out_0", (B * T, D), mybir.dt.float32, kind="ExternalOutput").ap())
    retention_moe_kernel(nc, *args)
    r = run_bass_kernel_spmd(nc, [{f"in_{n}": a for n, a in arrays.items()}], core_ids=[0])
    return r.results[0]["out_0"].reshape(B, T, D)
```

```python
import numpy as np
import concourse.bass as bass
from concourse import mybir
from contextlib import ExitStack

B, T, D = 2, 1024, 128
H, DH = 16, 8
NE, TOPK, HID = 8, 2, 352
EPS = 1e-5

P = 128
C = 64
NG = 4
HG = H // NG
PAIRS = T // P
TILES = T * TOPK // P + NE - 1
SLOTS = TILES * P
NT = B * TILES
HC = (HID + P - 1) // P
HP = HC * P
WCOLS = 2 * HP + HC * D

ROUTED = 14
EARLY = 10
COMBINED = 38

_CONST = [("ydecay", C), ("kdecay", 2 * D), ("sdecay", 2), ("headsel", HG), ("blockdiag", D), ("causal", NG * HG * C),
          ("headmean", D), ("ident", P), ("before", P), ("ones", P), ("rank_e", NE * PAIRS), ("tilestart", NE * NE),
          ("tileid", TILES * NE), ("half", PAIRS), ("answer_row", TOPK * PAIRS), ("blank_row", TILES)]
COL, _at = {}, 0
for _name, _n in _CONST:
    COL[_name] = (_at, _at + _n)
    _at += _n
NCONST = _at


def shape_constants():
    c = np.zeros((P, NCONST), np.float64)

    def put(name, a):
        c[:, COL[name][0]:COL[name][1]] = np.asarray(a, np.float64).reshape(a.shape[0], -1)

    gamma = 1.0 - 2.0 ** (-5.0 - np.arange(H))
    p = np.arange(P)
    s = p % C
    t = np.arange(C)
    g = gamma.reshape(1, NG, HG, 1)
    put("causal", np.where(t[None, None, None, :] >= s[:, None, None, None], g ** (-(s[:, None, None, None] + 1.0)), 0.0))
    head = p // DH
    put("ydecay", gamma[head][:, None] ** (t[None, :] + 1.0) / np.sqrt(DH))
    k0 = np.where(p[:, None] < C, gamma[head][None, :] ** (C - 1.0 - p[:, None]), 0.0)
    k1 = gamma[head][None, :] ** (2 * C - 1.0 - p[:, None])
    put("kdecay", np.stack([k0, k1], 1))
    put("sdecay", np.stack([gamma[head] ** C, gamma[head] ** (2 * C)], 1))
    put("headsel", (head % HG)[:, None] == np.arange(HG)[None, :])
    same = (head[:, None] == head[None, :]).astype(np.float64)
    put("blockdiag", same)
    put("headmean", same / DH)
    put("ident", np.eye(P))
    put("before", p[:, None] < p[None, :])
    put("ones", np.ones((P, P)))
    put("rank_e", np.broadcast_to(NE - np.arange(NE, dtype=float)[None, None, :], (P, PAIRS, NE)))
    put("tilestart", np.broadcast_to(P * np.arange(NE, dtype=float)[None, None, :], (P, NE, NE)))
    put("tileid", np.broadcast_to(np.arange(TILES, dtype=float)[None, :, None], (P, TILES, NE)))
    k, n = np.arange(TOPK)[None, :, None], np.arange(PAIRS)[None, None, :]
    put("answer_row", k * T + n * P + p[:, None, None])
    put("blank_row", TOPK * T + np.arange(TILES)[None, :] * P + p[:, None])
    put("half", np.full((P, PAIRS), -0.5))
    return c.astype(np.float32)


def retention_moe_kernel(nc, x_tok, x_T, wqT, wkT, wvT, woT, gnw, gnb, gateT, ebias, w1, w2, w3, const, out):
    f32, i32 = mybir.dt.float32, mybir.dt.int32
    ALU = mybir.AluOpType
    ACT = mybir.ActivationFunctionType
    AX = mybir.AxisListType.X

    routed = [nc.dram_tensor(f"routed_rows{b}", [SLOTS, D + 1], f32, kind="Internal").ap() for b in range(B)]
    answers = [nc.dram_tensor(f"answer_rows{b}", [TOPK * T + SLOTS, D], f32, kind="Internal").ap() for b in range(B)]

    ctx = ExitStack()
    with ctx:
        def sb(name, shape, dt=f32):
            return ctx.enter_context(nc.sbuf_tensor(name, shape, dt))

        def sem(name):
            return ctx.enter_context(nc.semaphore(name))

        cst = sb("cst", [P, NCONST])

        def const_of(name, rows=P):
            return cst[0:rows, COL[name][0]:COL[name][1]]

        causal = const_of("causal").rearrange("p (g n) -> p g n", g=NG)
        ydecay, kdecay = const_of("ydecay"), const_of("kdecay").rearrange("p (j n) -> p j n", j=2)
        sdecay, headsel = const_of("sdecay"), const_of("headsel")
        blockdiag, headmean, ident = const_of("blockdiag"), const_of("headmean"), const_of("ident")

        wq_s, wk_s, wv_s, wo_s = (sb(n, [P, D]) for n in ("wq_s", "wk_s", "wv_s", "wo_s"))
        gate_s = sb("gate_s", [P, NE])
        gn_s = sb("gn_s", [P, 2])
        eb_s = sb("eb_s", [P, NE])
        w_s = sb("w_s", [P, NE, WCOLS])
        xres = sb("xres", [P, B * PAIRS, D])
        
        warm = sb("warm", [P, 512], mybir.dt.bfloat16)
        hot = sb("hot", [P, 1])

        xT_all = sb("xT_all", [P, B * T])
        xt = sb("xt", [P, 2, P])
        qT, kT = sb("qT", [P, 2, P]), sb("kT", [P, 2, P])
        qx = sb("qx", [P, 2, HG, P])
        vx = sb("vx", [P, 2, H * 32])
        kd = sb("kd", [P, 2, 2, D])
        att = sb("att", [P, 2, NG, HG * C])
        um = sb("um", [P, 2, D])
        s0, s1 = sb("s0", [P, 2, D]), sb("s1", [P, 2, D])
        yT = sb("yT", [P, B * T])
        ystats = sb("ystats", [P, B * PAIRS, 6])
        gn = sb("gn", [P, 12])
        yn = sb("yn", [P, T])

        z = sb("z", [P, B * PAIRS, D])
        x1 = sb("x1", [P, B * PAIRS, D])
        x1T = sb("x1T", [P, PAIRS, P])
        lstats, lmv = sb("lstats", [P, PAIRS, 6]), sb("lmv", [P, PAIRS, 2])
        lvar, lrstd = sb("lvar", [P, PAIRS]), sb("lrstd", [P, PAIRS])
        rt = {n: sb("rt_" + n, [P, PAIRS, NE]) for n in ("d", "ex", "sc", "key", "eq", "oh1", "oh2", "w")}
        r8 = {n: sb("r8_" + n, [P, PAIRS]) for n in ("mx", "sum", "rc", "m", "f", "tot", "nt", "te", "ts", "off", "sl")}
        prob = sb("prob", [P, TOPK, PAIRS])
        ohe = sb("ohe", [P, NE, PAIRS])
        rank = sb("rank", [P, 2 * NE * PAIRS])
        cum = sb("cum", [P, NE * PAIRS + 1])
        pos = sb("pos", [P, NE, PAIRS])
        gtt = sb("gtt", [P, NE, NE])
        tcmp, tsum = sb("tcmp", [1, TILES, NE]), sb("tsum", [1, TILES])
        slot = sb("slot", [P, B, TOPK, PAIRS], i32)
        expert = sb("expert", [1, NT], i32)
        xs = sb("xs", [P, B, TOPK, PAIRS, D + 1])

        xg, xgT = sb("xg", [P, 2, D + 1]), sb("xgT", [P, 2, P])
        wt = sb("wt", [P, 2, 2 * HP])
        act_s, hT = sb("act_s", [P, 2, HP]), sb("hT", [P, 2, HP])
        yo = sb("yo", [P, NT * D])
        answer_row = sb("answer_row", [P, NT], i32)

        bank = [ctx.enter_context(nc.psum_tensor(f"bank{i}", [P, 512], f32)) for i in range(8)]

        s_qkv = sem("s_qkv")
        s_decay = sem("s_decay")
        s_causal = sem("s_causal")
        s_in = sem("s_in")
        warm_zero = sem("warm_zero")
        s_xres = sem("s_xres")
        s_moew = sem("s_moew")
        s_zero = sem("s_zero")
        blank_ready = sem("blank_ready")
        s_blank = sem("s_blank")
        s_xT = sem("s_xT")
        xt_done = sem("xt_done")
        qkv_done = sem("qkv_done")
        proj_done = sem("proj_done")
        projev_done = sem("projev_done")
        kd_done = sem("kd_done")
        scores_done = sem("scores_done")
        att_done = sem("att_done")
        u_done = sem("u_done")
        um_done = sem("um_done")
        st_done = sem("st_done")
        y_done = sem("y_done")
        yev_done = sem("yev_done")
        yst_done = sem("yst_done")
        dch = sem("dch")
        gnst = sem("gnst")
        gnpe = sem("gnpe")
        var_ready = sem("var_ready")
        rstd_done = sem("rstd_done")
        gnab_done = sem("gnab_done")
        yn_done = sem("yn_done")
        o_done = sem("o_done")
        z_done = sem("z_done")
        x1_done = sem("x1_done")
        x1t_pe = sem("x1t_pe")
        x1t_done = sem("x1t_done")
        logit_done = sem("logit_done")
        d_done = sem("d_done")
        exp_done = sem("exp_done")
        oh_done = sem("oh_done")
        rank_done = sem("rank_done")
        prob_done = sem("prob_done")
        rank_read = sem("rank_read")
        slot_done = sem("slot_done")
        table_done = sem("table_done")
        xs_done = sem("xs_done")
        scat_done = [sem(f"scat_done{b}") for b in range(B)]
        xg_loaded = [sem("xg_loaded0"), sem("xg_loaded1")]
        t1_done = sem("t1_done")
        xgT_done = sem("xgT_done")
        gate_done = sem("gate_done")
        up_done = sem("up_done")
        wt_done = sem("wt_done")
        silu_done = sem("silu_done")
        hid_done = sem("hid_done")
        down_done = sem("down_done")
        yo_done = sem("yo_done")
        row_known = sem("row_known")
        answered = [sem(f"answered{b}") for b in range(B)]
        back_done = [[sem(f"back_done{b}{h}") for h in range(2)] for b in range(B)]
        sum_done = sem("sum_done")
        out_ready = sem("out_ready")
        stored = sem("stored")

        N_IN = 6 * 16
        HALF = PAIRS // 2
        spare = [(bank[4], bank[5]), (bank[5], bank[7])]

        blank = yo[:, 0:TILES * (D + 1)].rearrange("p (n d) -> p n d", d=D + 1)

        block = ctx.enter_context(nc.Block())

        def bcast(ap, n):
            return ap.unsqueeze(2).broadcast_to([ap.shape[0], ap.shape[1], n])

        def vdiag(u):
            v = vx[:, u, :]
            step = v.ap[-1][0]
            return bass.AP(v.tensor, v.offset, [v.ap[0], [P * step, NG], [(32 + DH) * step, HG], [step, DH]])

        @block.sync
        def _(sp):
            sp.dma_start(xt[:, :, :].rearrange("p n t -> p (n t)"), x_T[:, 0:2 * P]).then_inc(s_qkv, 16)
            for dst, src in ((wq_s, wqT), (wk_s, wkT), (wv_s, wvT)):
                sp.dma_start(dst[:, :], src).then_inc(s_qkv, 16)
            c0, c1 = COL["causal"]
            sp.dma_start(cst[:, 0:c0], const[:, 0:c0]).then_inc(s_decay, 16)
            sp.dma_start(cst[:, c0:c1], const[:, c0:c1]).then_inc(s_causal, 16)
            sp.dma_start(xT_all[:, :], x_T).then_inc(s_xT, 16)
            sp.dma_start(cst[:, c1:NCONST], const[:, c1:NCONST]).then_inc(s_in, 16)
            for dst, src in ((wo_s, woT), (gate_s, gateT), (eb_s, ebias)):
                sp.dma_start(dst[:, :], src).then_inc(s_in, 16)
            sp.dma_start(gn_s[:, 0:1], gnw).then_inc(s_in, 16)
            sp.dma_start(gn_s[:, 1:2], gnb).then_inc(s_in, 16)
            sp.dma_start(xres[:, :, :], x_tok.rearrange("(n p) d -> p n d", p=P)).then_inc(s_xres, 16)

            def load_tile(b, n, u, reuse=True):
                if reuse:
                    sp.wait_ge(row_known, b * TILES + n - 1)
                sp.dma_start(xg[:, u, :], routed[b][bass.ds(n * P, P), :]).then_inc(xg_loaded[u], 16)

            def load_tiles(b, lo, hi):
                with sp.Fori(0, (hi - lo) // 2) as i:
                    for w in range(2):
                        load_tile(b, 2 * i + lo + w, (b * TILES + lo + w) % 2)

            def load_answers(b):
                sp.wait_ge(answered[b], 16 * TILES)
                for h in range(2):
                    for k in range(TOPK):
                        r0 = k * T + h * HALF * P
                        sp.dma_start(xs[:, b, k, h * HALF:(h + 1) * HALF, 0:D],
                                     answers[b][r0:r0 + HALF * P, :].rearrange("(n p) d -> p n d", p=P))\
                            .then_inc(back_done[b][h], 16)

            sp.wait_ge(blank_ready, 1)
            for b in range(B):
                sp.dma_start(routed[b].rearrange("(n p) d -> p n d", p=P), blank).then_inc(s_blank, 16)

            for b in range(B):
                sp.wait_ge(scat_done[b], 16 * TOPK * PAIRS)
                for n in range(3):
                    load_tile(b, n, (b * TILES + n) % 2, b > 0 or n > 1)
                if b == 0:
                    load_tiles(b, 3, TILES)
                else:
                    load_tiles(b, 3, COMBINED - 4 - TILES)
                    load_answers(0)
                    load_tiles(b, COMBINED - 4 - TILES, TILES)
            load_answers(1)

            for b in range(B):
                for h in range(2):
                    sp.wait_ge(out_ready, 2 * b + h + 1)
                    t0 = b * PAIRS + h * HALF
                    sp.dma_start(out.rearrange("(n p) d -> p n d", p=P)[:, t0:t0 + HALF, :],
                                 z[:, t0:t0 + HALF, :]).then_inc(stored, 16)
            sp.wait_ge(stored, 16 * 2 * B)

        @block.gpsimd
        def _(pool):
            for n, a in enumerate((vx[:, :, :], w_s[:, :, HID:HP], w_s[:, :, HP + HID:2 * HP],
                                   w_s[HID - (HC - 1) * P:P, :, WCOLS - D:WCOLS], cum[:, 0:1], blank)):
                pool.memset(a, 0.0).then_inc(s_zero, 1)
                pool.wait_ge(s_zero, n + 1)
            pool.wait_ge(s_in, N_IN)
            pool.tensor_copy(blank[:, :, D], const_of("blank_row")).then_inc(blank_ready, 1)

            def rstd(dst, src):
                pool.tensor_tensor(out=dst, in0=src, in1=const_of("half")[:, 0:dst.shape[1]], op=ALU.pow)\
                    .then_inc(rstd_done, 1)

            def scatter(b):
                for k in range(TOPK):
                    for n in range(PAIRS):
                        pool.wait_ge(xs_done, TOPK * PAIRS * b + k * PAIRS + n + 1)
                        pool.indirect_dma_start(
                            out=routed[b][:, :], out_offset=bass.IndirectOffsetOnAxis(ap=slot[:, b, k, n:n + 1], axis=0),
                            in_=xs[:, b, k, n, :], in_offset=None).then_inc(scat_done[b], 16)

            def deliver(b, lo, hi):
                for g in range(lo, hi):
                    pool.wait_ge(yo_done, g + 1)
                    pool.indirect_dma_start(
                        out=answers[b][:, :], out_offset=bass.IndirectOffsetOnAxis(ap=answer_row[:, g:g + 1], axis=0),
                        in_=yo[:, g * D:(g + 1) * D], in_offset=None).then_inc(answered[b], 16)

            def add_answers(b, h, first=0):
                n = slice(h * HALF + first, (h + 1) * HALF)
                t = slice(b * PAIRS + h * HALF + first, b * PAIRS + (h + 1) * HALF)
                pool.wait_ge(back_done[b][h], 16 * TOPK)
                pool.tensor_tensor(out=z[:, t, :], in0=xs[:, b, 0, n, 0:D], in1=xs[:, b, 1, n, 0:D], op=ALU.add)\
                    .then_inc(sum_done, 1)
                pool.wait_ge(sum_done, 2 * (b + h) + 1)
                pool.tensor_tensor(out=z[:, t, :], in0=z[:, t, :], in1=x1[:, t, :], op=ALU.add).then_inc(sum_done, 1)

            def rstd_halves(n_var):
                for h in range(2):
                    pool.wait_ge(var_ready, n_var + h)
                    rstd(lrstd[:, h * HALF:(h + 1) * HALF], lvar[:, h * HALF:(h + 1) * HALF])

            for b in range(B):
                pool.wait_ge(var_ready, 3 * b + 1)
                rstd(gn[:, 6:7], gn[:, 5:6])
                rstd_halves(3 * b + 2)
                if b == 1:
                    deliver(0, 0, EARLY)
                pool.wait_ge(slot_done, b + 1)
                if b == 0:
                    pool.wait_ge(s_blank, 16 * B)
                scatter(b)
            deliver(0, EARLY, TILES)
            deliver(1, TILES, COMBINED - 4)
            add_answers(0, 0)
            add_answers(0, 1)
            deliver(1, COMBINED - 4, COMBINED)
            rstd_halves(3 * B + 1)
            deliver(1, COMBINED, NT)
            add_answers(1, 1, HALF // 2)
            rstd_halves(3 * B + 3)

        @block.scalar
        def _(act):
            act.wait_ge(warm_zero, 1)
            nc.scalar.activation(hot[:, :], warm[:, 0:1], ACT.Copy)

            def evacuate(p, u, reuse=True):
                act.wait_ge(qkv_done, p + 1)
                if reuse:
                    act.wait_ge(y_done, p - 1)
                nc.scalar.copy(qT[:, u, :], bank[0][:, 0:P])
                nc.scalar.copy(kT[:, u, :], bank[0][:, P:2 * P])
                nc.scalar.copy(vdiag(u), bank[0][:, 2 * P:3 * P].rearrange("p (g i d) -> p g i d", g=NG, i=HG))
                if not reuse:
                    act.wait_ge(s_decay, 16)
                for i in range(HG):
                    last = nc.scalar.activation(qx[:, u, i, :], bank[0][:, 0:P], ACT.Copy, scale=headsel[:, i:i + 1])
                last.then_inc(projev_done, 1)

            def next_pair(p, u):
                act.wait_ge(proj_done, p + 1)
                nc.scalar.copy(xt[:, u, :], xT_all[:, bass.ds((p + 2) * P, P)]).then_inc(xt_done, 1)

            def load_expert_weights():
                act.dma_start(w_s[:, :, 0:HID], w1.rearrange("e p n -> p e n")).then_inc(s_moew, 16)
                act.dma_start(w_s[:, :, HP:HP + HID], w3.rearrange("e p n -> p e n")).then_inc(s_moew, 16)
                for c in range(HC):
                    rows = min(P, HID - c * P)
                    act.dma_start(w_s[0:rows, :, 2 * HP + c * D:2 * HP + (c + 1) * D],
                                  w2[:, c * P:c * P + rows, :].rearrange("e p n -> p e n"))\
                        .then_inc(s_moew, 16)

            def norm_y(b):
                act.wait_ge(gnab_done, b + 1)
                if b > 0:
                    act.wait_ge(o_done, 2 * b)
                for h in range(2):
                    t0 = b * T + h * HALF * P
                    nc.scalar.activation(yn[:, h * HALF * P:(h + 1) * HALF * P], yT[:, t0:t0 + HALF * P], ACT.Identity,
                                         scale=gn[:, 7:8], bias=gn[:, 9:10]).then_inc(yn_done, 1)

            def x1_T(b, h):
                act.wait_ge(x1t_pe, 2 * b + h + 1)
                if b > 0 and h == 0:
                    act.wait_ge(logit_done, b)
                nc.scalar.copy(x1T[:, h * HALF:(h + 1) * HALF, :],
                               spare[b][h][:, :].rearrange("p (n d) -> p n d", n=HALF)).then_inc(x1t_done, 1)

            def exp_logits(b):
                act.wait_ge(d_done, b + 1)
                nc.scalar.activation(rt["ex"][:, :, :], rt["d"][:, :, :], ACT.Exp).then_inc(exp_done, 1)

            def weigh_rows(b, k, h):
                act.wait_ge(prob_done, b + 1)
                for n in range(h * HALF, (h + 1) * HALF):
                    nc.scalar.activation(xs[:, b, k, n, 0:D], x1[:, b * PAIRS + n, :], ACT.Copy,
                                         scale=prob[:, k, n:n + 1]).then_inc(xs_done, 1)

            act.wait_ge(s_zero, 5)
            evacuate(0, 0, False)
            act.wait_ge(s_xT, 16)
            next_pair(0, 0)
            evacuate(1, 1, False)
            next_pair(1, 1)
            load_expert_weights()
            with act.Fori(0, PAIRS // 2 - 1) as i:
                for u in range(2):
                    evacuate(2 + 2 * i + u, u)
                    next_pair(2 + 2 * i + u, u)
            for n in range(PAIRS):
                evacuate(PAIRS + n, n % 2)
                if n == 0:
                    norm_y(0)
                if n < PAIRS - 2:
                    next_pair(PAIRS + n, n % 2)
                if n == 2:
                    x1_T(0, 0)
                elif n == 3:
                    x1_T(0, 1)
                    exp_logits(0)
                elif n in (5, 6):
                    weigh_rows(0, n - 5, 0)
                    weigh_rows(0, n - 5, 1)

            w_flat = w_s[:, :, :].rearrange("p e n -> p (e n)")
            expert_at = [act.alloc_register(f"weights_of_tile{u}") for u in range(2)]

            def fetch_weights(g, u):
                act.reg_load(expert_at[u], expert[0:1, bass.ds(g, 1)])
                at = act.snap(expert_at[u], min_val=0, max_val=(NE - 1) * WCOLS)
                nc.scalar.copy(wt[:, u, :], w_flat[:, bass.ds(at, 2 * HP)]).then_inc(wt_done, 1)

            def silu(g, u, reuse=True):
                act.wait_ge(gate_done, g + 1)
                if reuse:
                    act.wait_ge(hid_done, g - 1)
                nc.scalar.activation(act_s[:, u, :], bank[1 + u][:, 0:HP], ACT.Silu).then_inc(silu_done, 1)

            def note_rows(g, u):
                act.wait_ge(t1_done, g + 1)
                nc.scalar.copy(answer_row[:, bass.ds(g, 1)], xg[:, u, D:D + 1]).then_inc(row_known, 1)

            def tile_step(g, u):
                silu(g, u)
                act.wait_ge(up_done, g + 1)
                note_rows(g + 2, u)
                fetch_weights(g + 2, u)

            def tile_steps(lo, hi):
                with act.Fori(0, (hi - lo) // 2) as i:
                    for u in range(2):
                        tile_step(2 * i + lo + u, u)

            act.wait_ge(s_moew, 16 * (2 + HC))
            act.wait_ge(table_done, 1)
            fetch_weights(0, 0)
            fetch_weights(1, 1)
            note_rows(0, 0)
            note_rows(1, 1)
            norm_y(1)
            for g in range(2):
                silu(g, g, False)
                act.wait_ge(up_done, g + 1)
                note_rows(g + 2, g)
                fetch_weights(g + 2, g)
            for g in range(2, ROUTED):
                tile_step(g, g % 2)
                if g == 5:
                    x1_T(1, 0)
                elif g == 6:
                    x1_T(1, 1)
                    exp_logits(1)
                elif g == 9:
                    weigh_rows(1, 0, 0)
                elif g == 10:
                    weigh_rows(1, 0, 1)
                    weigh_rows(1, 1, 0)
                elif g == 11:
                    weigh_rows(1, 1, 1)
            tile_steps(ROUTED, TILES - 3)
            act.wait_ge(table_done, 2)
            tile_steps(TILES - 3, NT - 2)
            silu(NT - 2, 0)
            silu(NT - 1, 1)

        @block.vector
        def _(dve):
            chain = [0]

            def link(ins):
                chain[0] += 1
                ins.then_inc(dch, 1)
                dve.wait_ge(dch, chain[0])

            V = nc.vector

            def decay_k(p, u):
                dve.wait_ge(proj_done, p + 1)
                V.tensor_tensor(out=kd[:, u, :, :], in0=bank[1][:, 0:D].unsqueeze(1).broadcast_to([P, 2, D]),
                                in1=kdecay, op=ALU.mult).then_inc(kd_done, 1)

            def decay_scores(p, u):
                for half in range(2):
                    dve.wait_ge(scores_done, 2 * p + half + 1)
                    for g in (2 * half, 2 * half + 1):
                        ins = V.tensor_tensor(out=att[:, u, g, :], in0=bank[2 + g][:, 0:HG * C],
                                              in1=causal[:, g, :], op=ALU.mult)
                    ins.then_inc(att_done, 1)

            def states(p, u):
                dve.wait_ge(u_done, p + 1)
                V.tensor_tensor(out=um[:, :, :], in0=bank[1][:, P:3 * P].rearrange("p (j n) -> p j n", j=2),
                                in1=blockdiag.unsqueeze(1).broadcast_to([P, 2, D]), op=ALU.mult).then_inc(um_done, 1)
                dve.wait_ge(um_done, p + 1)
                dve.wait_ge(y_done, p)
                V.scalar_tensor_tensor(out=s1[:, u, :], in0=s0[:, u, :], scalar=sdecay[:, 0:1], in1=um[:, 0, :],
                                       op0=ALU.mult, op1=ALU.add)
                V.scalar_tensor_tensor(out=s0[:, 1 - u, :], in0=s0[:, u, :], scalar=sdecay[:, 1:2], in1=um[:, 1, :],
                                       op0=ALU.mult, op1=ALU.add).then_inc(st_done, 1)
                dve.wait_ge(st_done, p + 1)

            def evacuate_y(p):
                dve.wait_ge(y_done, p + 1)
                for j in range(2):
                    ins = V.tensor_tensor(out=yT[:, bass.ds(p * P + j * C, C)], in0=bank[6 + j][:, 0:C], in1=ydecay,
                                          op=ALU.mult)
                ins.then_inc(yev_done, 1)
                dve.wait_ge(yev_done, p + 1)
                V.bn_stats(out=ystats[:, :, :].rearrange("p n s -> p (n s)")[:, bass.ds(p * 6, 6)],
                           in_=yT[:, bass.ds(p * P, P)]).then_inc(yst_done, 1)

            def norm_stats(b, h):
                halves = range(h * HALF, (h + 1) * HALF)
                for n in halves:
                    ins = V.bn_stats(out=lstats[:, n, :], in_=z[:, b * PAIRS + n, :])
                link(ins)
                for n in halves:
                    ins = V.bn_aggr(out=lmv[:, n, :], in_=lstats[:, n, :])
                link(ins)
                V.tensor_scalar(lvar[:, halves[0]:halves[-1] + 1], lmv[:, halves[0]:halves[-1] + 1, 1], EPS, None, ALU.add)\
                    .then_inc(var_ready, 1)

            def norm_apply(b, h, dst, n_var, done):
                dve.wait_ge(rstd_done, n_var)
                for n in range(h * HALF, (h + 1) * HALF):
                    ins = V.tensor_scalar(dst[:, b * PAIRS + n, :], z[:, b * PAIRS + n, :], lmv[:, n, 0:1],
                                          lrstd[:, n:n + 1], ALU.subtract, ALU.mult)
                ins.then_inc(done, 1)

            def group_norm(b):
                dve.wait_ge(yst_done, (b + 1) * PAIRS)
                V.bn_aggr(out=gn[:, 0:2], in_=ystats[:, b * PAIRS:(b + 1) * PAIRS, :].rearrange("p n s -> p (n s)"))\
                    .then_inc(gnst, 1)
                sums = spare[b][1]
                dve.wait_ge(gnpe, 2 * b + 1)
                link(V.tensor_copy(gn[:, 2:4], sums[:, 0:2]))
                link(V.tensor_tensor(out=gn[:, 11:12], in0=gn[:, 0:1], in1=gn[:, 2:3], op=ALU.subtract))
                V.tensor_tensor(out=gn[:, 4:5], in0=gn[:, 11:12], in1=gn[:, 11:12], op=ALU.mult).then_inc(gnst, 1)
                dve.wait_ge(gnpe, 2 * b + 2)
                V.scalar_tensor_tensor(out=gn[:, 5:6], in0=sums[:, 2:3], scalar=EPS, in1=gn[:, 3:4],
                                       op0=ALU.add, op1=ALU.add).then_inc(var_ready, 1)
                dve.wait_ge(rstd_done, 3 * b + 1)
                link(V.tensor_tensor(out=gn[:, 7:8], in0=gn[:, 6:7], in1=gn_s[:, 0:1], op=ALU.mult))
                link(V.tensor_tensor(out=gn[:, 8:9], in0=gn[:, 2:3], in1=gn[:, 7:8], op=ALU.mult))
                V.tensor_tensor(out=gn[:, 9:10], in0=gn_s[:, 1:2], in1=gn[:, 8:9], op=ALU.subtract).then_inc(gnab_done, 1)

            def residual(b, h):
                dve.wait_ge(o_done, 2 * b + h + 1)
                t0 = b * PAIRS + h * HALF
                V.tensor_tensor(out=z[:, t0:t0 + HALF, :], in0=spare[b][h][:, :].rearrange("p (n d) -> p n d", n=HALF),
                                in1=xres[:, t0:t0 + HALF, :], op=ALU.add).then_inc(z_done, 1)

            t3 = {n: a[:, :, :] for n, a in rt.items()}
            desc = const_of("rank_e").rearrange("p (n e) -> p n e", e=NE)
            n64 = NE * PAIRS

            def read_logits(b):
                logits = spare[b][0][:, 0:n64].rearrange("p (n e) -> p n e", e=NE)
                dve.wait_ge(logit_done, b + 1)
                link(V.tensor_reduce(r8["mx"][:, :], logits, AX, ALU.max))
                V.tensor_tensor(out=t3["d"], in0=logits, in1=bcast(r8["mx"][:, :], NE), op=ALU.subtract).then_inc(d_done, 1)

            def softmax(b):
                dve.wait_ge(exp_done, b + 1)
                link(V.tensor_reduce(r8["sum"][:, :], t3["ex"], AX, ALU.add))
                link(V.reciprocal(r8["rc"][:, :], r8["sum"][:, :]))
                link(V.tensor_tensor(out=t3["sc"], in0=t3["ex"], in1=bcast(r8["rc"][:, :], NE), op=ALU.mult))
                link(V.tensor_tensor(out=t3["key"], in0=t3["sc"],
                                     in1=eb_s[:, :].unsqueeze(1).broadcast_to([P, PAIRS, NE]), op=ALU.add))

            def choose(k):
                oh = t3[f"oh{k + 1}"]
                link(V.tensor_reduce(r8["m"][:, :], t3["key"], AX, ALU.max))
                link(V.tensor_tensor(out=t3["eq"], in0=t3["key"], in1=bcast(r8["m"][:, :], NE), op=ALU.is_equal))
                link(V.tensor_tensor(out=t3["w"], in0=t3["eq"], in1=desc, op=ALU.mult))
                link(V.tensor_reduce(r8["f"][:, :], t3["w"], AX, ALU.max))
                link(V.tensor_tensor(out=oh, in0=desc, in1=bcast(r8["f"][:, :], NE), op=ALU.is_equal))
                if k == 0:
                    link(V.scalar_tensor_tensor(out=t3["key"], in0=oh, scalar=-3e38, in1=t3["key"],
                                                op0=ALU.mult, op1=ALU.add))
                else:
                    V.tensor_tensor(out=ohe[:, :, :].rearrange("p e n -> p n e"), in0=t3["oh1"], in1=t3["oh2"],
                                    op=ALU.add).then_inc(oh_done, 1)

            def chosen_scores():
                for k in range(TOPK):
                    link(V.tensor_tensor(out=t3["w"], in0=t3["sc"], in1=t3[f"oh{k + 1}"], op=ALU.mult))
                    ins = V.tensor_reduce(prob[:, k, :], t3["w"], AX, ALU.add)
                    if k == 0:
                        link(ins)
                ins.then_inc(prob_done, 1)

            within, counts = rank[:, 0:n64], rank[:, n64:2 * n64]
            flat_pos = pos[:, :, :].rearrange("p e n -> p (e n)")

            def read_ranks(b):
                dve.wait_ge(rank_done, b + 1)
                V.tensor_copy(rank[:, :], spare[b][1][:, 0:2 * n64]).then_inc(rank_read, 1)
                dve.wait_ge(rank_read, b + 1)

            def expert_starts():
                link(V.tensor_tensor_scan(cum[:, 1:n64 + 1], const_of("ones")[:, 0:n64], counts, 0.0, ALU.mult, ALU.add))
                link(V.tensor_tensor(out=flat_pos, in0=cum[:, 1:n64 + 1], in1=counts, op=ALU.subtract))
                starts, ends = cum[:, 0:n64:PAIRS], cum[:, PAIRS:n64 + 1:PAIRS]
                link(V.tensor_tensor(out=r8["tot"][:, :], in0=ends, in1=starts, op=ALU.subtract))
                link(V.tensor_tensor(out=gtt[:, :, :], in0=bcast(r8["tot"][:, :], NE),
                                     in1=const_of("tilestart").rearrange("p (e j) -> p e j", j=NE), op=ALU.is_gt))
                link(V.tensor_reduce(r8["nt"][:, :], gtt[:, :, :], AX, ALU.add))
                link(V.tensor_tensor_scan(r8["te"][:, :], const_of("ones")[:, 0:NE], r8["nt"][:, :], 0.0, ALU.mult, ALU.add))
                link(V.tensor_tensor(out=r8["ts"][:, :], in0=r8["te"][:, :], in1=r8["nt"][:, :], op=ALU.subtract))
                link(V.scalar_tensor_tensor(out=r8["off"][:, :], in0=r8["ts"][:, :], scalar=float(P), in1=starts,
                                            op0=ALU.mult, op1=ALU.subtract))

            def slots(b):
                link(V.tensor_tensor(out=pos[:, :, :], in0=pos[:, :, :], in1=bcast(r8["off"][:, :], PAIRS), op=ALU.add))
                link(V.tensor_tensor(out=flat_pos, in0=flat_pos, in1=within, op=ALU.add))
                for k in range(TOPK):
                    link(V.tensor_tensor(out=t3["w"], in0=t3[f"oh{k + 1}"], in1=pos[:, :, :].rearrange("p e n -> p n e"),
                                         op=ALU.mult))
                    link(V.tensor_reduce(r8["sl"][:, :], t3["w"], AX, ALU.add))
                    ins = V.tensor_copy(slot[:, b, k, :], r8["sl"][:, :])
                    if k == 0:
                        link(ins)
                ins.then_inc(slot_done, 1)

            def expert_table(b):
                link(V.tensor_tensor(out=tcmp[:, :, :], in0=const_of("tileid", 1).rearrange("p (g e) -> p g e", e=NE),
                                     in1=r8["te"][0:1, :].unsqueeze(1).broadcast_to([1, TILES, NE]), op=ALU.is_ge))
                link(V.tensor_reduce(tsum[:, :], tcmp[:, :, :], AX, ALU.add))
                V.tensor_scalar(expert[:, b * TILES:(b + 1) * TILES], tsum[:, :], float(NE - 1), float(WCOLS),
                                ALU.min, ALU.mult).then_inc(table_done, 1)

            def pair_head(p, u):
                evacuate_y(p - 1)
                decay_scores(p, u)
                states(p, u)

            def pair_step(p, u):
                pair_head(p, u)
                decay_k(p + 1, 1 - u)

            V.memset(warm[:, :], 0.0).then_inc(warm_zero, 1)
            dve.wait_ge(s_zero, 5)
            link(V.memset(s0[:, 0, :], 0.0))
            dve.wait_ge(s_decay, 16)
            decay_k(0, 0)
            dve.wait_ge(s_causal, 16)
            decay_scores(0, 0)
            states(0, 0)
            decay_k(1, 1)
            with dve.Fori(0, PAIRS // 2 - 1) as i:
                for w in range(2):
                    pair_step(2 * i + 1 + w, (1 + w) % 2)
            evacuate_y(PAIRS - 2)
            decay_scores(PAIRS - 1, 1)
            states(PAIRS - 1, 1)
            evacuate_y(PAIRS - 1)
            dve.wait_ge(s_in, N_IN)
            for b in range(B):
                V.tensor_copy(xs[:, b, :, :, D], const_of("answer_row").rearrange("p (k n) -> p k n", k=TOPK))
            group_norm(0)
            p1 = PAIRS
            link(V.memset(s0[:, 0, :], 0.0))
            decay_k(p1, 0)
            decay_scores(p1, 0)
            states(p1, 0)
            decay_k(p1 + 1, 1)
            dve.wait_ge(s_xres, 16)
            residual(0, 0)
            residual(0, 1)
            dve.wait_ge(z_done, 1)
            norm_stats(0, 0)
            pair_head(p1 + 1, 1)
            norm_apply(0, 0, x1, 2, x1_done)
            dve.wait_ge(z_done, 2)
            norm_stats(0, 1)
            decay_k(p1 + 2, 0)
            pair_head(p1 + 2, 0)
            norm_apply(0, 1, x1, 3, x1_done)
            decay_k(p1 + 3, 1)
            read_logits(0)
            softmax(0)
            choose(0)
            pair_head(p1 + 3, 1)
            choose(1)
            decay_k(p1 + 4, 0)
            chosen_scores()
            read_ranks(0)
            expert_starts()
            pair_head(p1 + 4, 0)
            slots(0)
            decay_k(p1 + 5, 1)
            pair_head(p1 + 5, 1)
            expert_table(0)
            decay_k(p1 + 6, 0)
            pair_step(p1 + 6, 0)
            evacuate_y(p1 + 6)
            decay_scores(p1 + 7, 1)
            states(p1 + 7, 1)
            evacuate_y(p1 + 7)
            group_norm(1)

            def rows_T(g, u):
                dve.wait_ge(t1_done, g + 1)
                V.tensor_copy(xgT[:, u, :], bank[0][:, 0:P]).then_inc(xgT_done, 1)

            def hidden(g, u):
                dve.wait_ge(silu_done, g + 1)
                dve.wait_ge(up_done, g + 1)
                V.tensor_tensor(out=hT[:, u, :], in0=bank[3 + u][:, 0:HP], in1=act_s[:, u, :], op=ALU.mult)\
                    .then_inc(hid_done, 1)

            def answer(g, down_bank=bank[6]):
                dve.wait_ge(down_done, g + 1)
                V.tensor_copy(yo[:, bass.ds(g * D, D)], down_bank[:, 0:D]).then_inc(yo_done, 1)

            def combine(b, h, tiles=HALF):
                dve.wait_ge(back_done[b][h], 16 * TOPK)
                n = slice(h * HALF, h * HALF + tiles)
                t = slice(b * PAIRS + h * HALF, b * PAIRS + h * HALF + tiles)
                link(V.tensor_tensor(out=z[:, t, :], in0=xs[:, b, 0, n, 0:D], in1=xs[:, b, 1, n, 0:D], op=ALU.add))
                link(V.tensor_tensor(out=z[:, t, :], in0=z[:, t, :], in1=x1[:, t, :], op=ALU.add))

            def tile_step(g, u):
                hidden(g, u)
                answer(g - 1)
                rows_T(g + 2, u)

            def tile_steps(lo, hi):
                with dve.Fori(0, (hi - lo) // 2) as i:
                    for u in range(2):
                        tile_step(2 * i + lo + u, u)

            rows_T(0, 0)
            rows_T(1, 1)
            hidden(0, 0)
            rows_T(2, 0)
            for g in range(1, ROUTED):
                tile_step(g, g % 2)
                if g == 1:
                    residual(1, 0)
                    residual(1, 1)
                elif g == 2:
                    dve.wait_ge(z_done, 3)
                    norm_stats(1, 0)
                elif g == 3:
                    dve.wait_ge(z_done, 4)
                    norm_stats(1, 1)
                elif g == 4:
                    norm_apply(1, 0, x1, 5, x1_done)
                elif g == 5:
                    norm_apply(1, 1, x1, 6, x1_done)
                elif g == 6:
                    read_logits(1)
                    softmax(1)
                elif g == 7:
                    choose(0)
                elif g == 8:
                    choose(1)
                elif g == 9:
                    chosen_scores()
                    read_ranks(1)
                    expert_starts()
                elif g == 10:
                    slots(1)
                elif g == 12:
                    expert_table(1)
            tile_steps(ROUTED, COMBINED)
            dve.wait_ge(sum_done, 2)
            norm_stats(0, 0)
            tile_step(COMBINED, 0)
            dve.wait_ge(sum_done, 4)
            norm_stats(0, 1)
            tile_step(COMBINED + 1, 1)
            norm_apply(0, 0, z, 3 * B + 1, out_ready)
            tile_step(COMBINED + 2, 0)
            norm_apply(0, 1, z, 3 * B + 2, out_ready)
            tile_step(COMBINED + 3, 1)
            tile_steps(COMBINED + 4, NT - 2)
            hidden(NT - 2, 0)
            answer(NT - 3)
            hidden(NT - 1, 1)
            answer(NT - 2)
            answer(NT - 1, bank[7])
            combine(1, 0)
            norm_stats(1, 0)
            combine(1, 1, HALF // 2)
            dve.wait_ge(sum_done, 6)
            norm_stats(1, 1)
            for h in range(2):
                norm_apply(B - 1, h, z, 3 * B + 2 + h + 1, out_ready)

        @block.tensor
        def _(pe):
            MM = nc.tensor.matmul

            def keep_warm(rounds):
                with pe.Fori(0, rounds):
                    for _ in range(4):
                        MM(bank[7][:, :], warm[:, 0:P], warm[:, :], start=True, stop=True)

            def fill(dst, n):
                for _ in range(n):
                    MM(dst, warm[:, 0:P], warm[:, 0:dst.shape[1]], start=True, stop=True)

            idle = slice(HG * C, 2 * HG * C)
            pe.wait_ge(warm_zero, 1)
            keep_warm(3)
            pe.wait_ge(s_qkv, 16 * 4)
            pe.wait_ge(s_zero, 5)

            def project(p, u, p_loaded=True):
                x = xt[:, u, :]
                if p_loaded:
                    pe.wait_ge(xt_done, p - 1)
                pe.wait_ge(projev_done, p)
                MM(bank[0][:, 0:P], wq_s[:, :], x, start=True, stop=True)
                MM(bank[0][:, P:2 * P], wk_s[:, :], x, start=True, stop=True)
                MM(bank[0][:, 2 * P:3 * P], x, wv_s[:, :], start=True, stop=True).then_inc(qkv_done, 1)

            def project_k(p, u):
                pe.wait_ge(um_done, p)
                MM(bank[1][:, 0:D], xt[:, u, :], wk_s[:, :], start=True, stop=True).then_inc(proj_done, 1)

            def scores(p, u, spare_read=None):
                pe.wait_ge(projev_done, p + 1)
                if spare_read is not None:
                    fill(bank[2][:, idle], spare_read[2])
                for half in range(2):
                    if half and spare_read is not None:
                        pe.wait_ge(spare_read[0], spare_read[1])
                    for j, gg in ((0, 0), (1, 1), (1, 0), (0, 1)):
                        g = 2 * half + gg
                        if gg == j:
                            fill(bank[2 + g][:, idle], 1)
                        r = slice(32 * g, 32 * g + 32)
                        c = slice(C * j, C * j + C)
                        last = MM(bank[2 + g][c, 0:HG * C], kT[r, u, c], qx[r, u, :, c], start=True, stop=True)
                    last.then_inc(scores_done, 1)

            def increments(p, u):
                pe.wait_ge(kd_done, p + 1)
                for j in range(2):
                    last = MM(bank[1][:, (1 + j) * P:(2 + j) * P], kd[:, u, j, :], vdiag(u), start=True, stop=True)
                last.then_inc(u_done, 1)

            def intra(p, u):
                pe.wait_ge(att_done, 2 * p + 2)
                pe.wait_ge(yev_done, p)
                fill(bank[2][:, idle], 1)
                for i in range(HG):
                    for g in range(NG):
                        for j in range(2):
                            c = slice(C * j, C * j + C)
                            h = g * HG + i
                            MM(bank[6 + j][32 * g:32 * g + 32, 0:C], vx[c, u, 32 * h:32 * h + 32],
                               att[c, u, g, i * C:(i + 1) * C], start=i == 0, stop=False, skip_group_check=True)

            def inter(p, u):
                pe.wait_ge(st_done, p + 1)
                for j, s in enumerate((s0, s1)):
                    last = MM(bank[6 + j][:, 0:C], s[:, u, :], qT[:, u, C * j:C * j + C], start=False, stop=True,
                              skip_group_check=True)
                last.then_inc(y_done, 1)

            def pair_rest(p, u):
                increments(p, u)
                project(p + 1, 1 - u, p > 0 if isinstance(p, int) else True)
                intra(p, u)
                project_k(p + 1, 1 - u)
                inter(p, u)

            def pair_step(p, u, spare_read=None):
                scores(p, u, spare_read)
                pair_rest(p, u)

            def head_means(b):
                sums = spare[b][1]
                fill(bank[2][:, idle], 8)
                pe.wait_ge(gnst, 2 * b + 1)
                MM(sums[:, 0:2], headmean, gn[:, 0:2], start=True, stop=True).then_inc(gnpe, 1)
                fill(bank[2][:, idle], 6)
                pe.wait_ge(gnst, 2 * b + 2)
                MM(sums[:, 2:3], headmean, gn[:, 4:5], start=True, stop=True).then_inc(gnpe, 1)

            def project_y(b, h):
                pe.wait_ge(yn_done, 2 * b + h + 1)
                for n in range(HALF):
                    t0 = (h * HALF + n) * P
                    last = MM(spare[b][h][:, n * D:(n + 1) * D], yn[:, t0:t0 + P], wo_s[:, :], start=True, stop=True)
                last.then_inc(o_done, 1)

            def transpose_x1(b, h):
                pe.wait_ge(x1_done, 2 * b + h + 1)
                for n in range(h * HALF, (h + 1) * HALF):
                    last = nc.tensor.transpose(spare[b][h][:, (n % HALF) * P:(n % HALF + 1) * P],
                                               x1[:, b * PAIRS + n, :], ident)
                last.then_inc(x1t_pe, 1)

            def router_logits(b):
                for n in range(PAIRS):
                    if n == 0:
                        pe.wait_ge(x1t_done, 2 * b + 1)
                    elif n == HALF:
                        pe.wait_ge(x1t_done, 2 * b + 2)
                    last = MM(spare[b][0][:, n * NE:(n + 1) * NE], x1T[:, n, :], gate_s[:, :], start=True, stop=True)
                last.then_inc(logit_done, 1)

            def ranks(b):
                pe.wait_ge(oh_done, b + 1)
                n64 = NE * PAIRS
                o = ohe[:, :, :].rearrange("p e n -> p (e n)")
                MM(spare[b][1][:, 0:n64], const_of("before"), o, start=True, stop=True)
                MM(spare[b][1][:, n64:2 * n64], const_of("ones"), o, start=True, stop=True).then_inc(rank_done, 1)

            project(0, 0, False)
            project_k(0, 0)
            keep_warm(1)
            scores(0, 0)
            pair_rest(0, 0)
            with pe.Fori(0, PAIRS // 2 - 1) as i:
                for w in range(2):
                    pair_step(2 * i + 1 + w, (1 + w) % 2)
            scores(PAIRS - 1, 1)
            increments(PAIRS - 1, 1)
            intra(PAIRS - 1, 1)
            inter(PAIRS - 1, 1)
            p1 = PAIRS
            project(p1, 0)
            project_k(p1, 0)
            pe.wait_ge(s_in, N_IN)
            head_means(0)
            scores(p1, 0, (var_ready, 1, 0))
            pair_rest(p1, 0)
            project_y(0, 0)
            project_y(0, 1)
            pair_step(p1 + 1, 1, (z_done, 2, 8))
            transpose_x1(0, 0)
            pair_step(p1 + 2, 0, (x1t_done, 1, 0))
            transpose_x1(0, 1)
            router_logits(0)
            pair_step(p1 + 3, 1, (d_done, 1, 12))
            ranks(0)
            pair_step(p1 + 4, 0, (rank_read, 1, 8))
            pair_step(p1 + 5, 1)
            pair_step(p1 + 6, 0)
            scores(p1 + 7, 1)
            increments(p1 + 7, 1)
            intra(p1 + 7, 1)
            inter(p1 + 7, 1)
            head_means(1)

            w_flat = w_s[:, :, :].rearrange("p e n -> p (e n)")
            expert_at = [pe.alloc_register(f"expert_of_tile{u}") for u in range(2)]

            def transpose_rows(g, u, n_loaded):
                pe.wait_ge(xg_loaded[u], n_loaded)
                pe.wait_ge(xgT_done, g)
                nc.tensor.transpose(bank[0][:, 0:P], xg[:, u, 0:D], ident).then_inc(t1_done, 1)

            def gate_up(g, u):
                pe.wait_ge(wt_done, g + 1)
                for w, done in enumerate((gate_done, up_done)):
                    for c in range(HC):
                        last = MM(bank[1 + 2 * w + u][:, c * P:(c + 1) * P],
                                  wt[:, u, w * HP + c * P:w * HP + (c + 1) * P], xgT[:, u, :], start=True, stop=True)
                    last.then_inc(done, 1)

            def weights_of(g, u):
                pe.reg_load(expert_at[u], expert[0:1, bass.ds(g, 1)])
                return pe.snap(expert_at[u], min_val=0, max_val=(NE - 1) * WCOLS)

            def down(g, u, at, down_bank=bank[6]):
                pe.wait_ge(hid_done, g + 1)
                for c in range(HC):
                    last = MM(down_bank[:, 0:D], hT[:, u, c * P:(c + 1) * P], w_flat[:, bass.ds(at + (2 * HP + c * D), D)],
                              start=c == 0, stop=c == HC - 1)
                last.then_inc(down_done, 1)

            def tile_step(g, half, u):
                at = weights_of(g - 1, 1 - u)
                gate_up(g, u)
                transpose_rows(g + 2, u, 16 * (half + 2))
                down(g - 1, 1 - u, at)

            def tile_steps(lo, hi):
                assert (hi - lo) % 6 == 0
                with pe.Fori(0, (hi - lo) // 6) as i:
                    for w in range(6):
                        tile_step(6 * i + lo + w, 3 * i + (lo + w) // 2, w % 2)

            transpose_rows(0, 0, 16)
            transpose_rows(1, 1, 16)
            gate_up(0, 0)
            transpose_rows(2, 0, 32)
            project_y(1, 0)
            for g in range(1, ROUTED):
                tile_step(g, g // 2, g % 2)
                if g == 1:
                    project_y(1, 1)
                elif g == 5:
                    transpose_x1(1, 0)
                elif g == 6:
                    transpose_x1(1, 1)
                    router_logits(1)
                elif g == 9:
                    ranks(1)
            tile_steps(ROUTED, TILES - 3)
            pe.wait_ge(table_done, 2)
            tile_steps(TILES - 3, NT - 2)
            gate_up(NT - 2, 0)
            pe.wait_ge(xgT_done, NT)
            down(NT - 3, 1, weights_of(NT - 3, 1))
            gate_up(NT - 1, 1)
            pe.wait_ge(yo_done, NT - 2)
            down(NT - 2, 0, weights_of(NT - 2, 0))
            down(NT - 1, 1, weights_of(NT - 1, 1), bank[7])


def kernel(L0_attn_x, L0_attn_W_q, L0_attn_W_k, L0_attn_W_v, L0_attn_W_o, L0_attn_gn_weight, L0_attn_gn_bias,
           L0_ffn_gate_w, L0_ffn_expert_bias, L0_ffn_w1, L0_ffn_w2, L0_ffn_w3):
    import concourse.bacc as bacc
    from concourse.bass_utils import run_bass_kernel_spmd

    def lay(a):
        return np.ascontiguousarray(a)

    x = np.asarray(L0_attn_x).reshape(B * T, D)
    arrays = {
        "x_tok": lay(x), "x_T": lay(x.T),
        "wqT": lay(np.asarray(L0_attn_W_q).T), "wkT": lay(np.asarray(L0_attn_W_k).T),
        "wvT": lay(np.asarray(L0_attn_W_v).T), "woT": lay(np.asarray(L0_attn_W_o).T),
        "gnw": lay(np.asarray(L0_attn_gn_weight).reshape(D, 1)), "gnb": lay(np.asarray(L0_attn_gn_bias).reshape(D, 1)),
        "gateT": lay(np.asarray(L0_ffn_gate_w).T),
        "ebias": lay(np.broadcast_to(np.asarray(L0_ffn_expert_bias)[None, :], (P, NE))),
        "w1": lay(L0_ffn_w1), "w2": lay(L0_ffn_w2), "w3": lay(L0_ffn_w3),
        "const": shape_constants(),
    }
    nc = bacc.Bacc("TRN2", target_bir_lowering=False, num_devices=1)
    args = [nc.dram_tensor(f"in_{n}", a.shape, mybir.dt.from_np(a.dtype), kind="ExternalInput").ap()
            for n, a in arrays.items()]
    args.append(nc.dram_tensor("out_0", (B * T, D), mybir.dt.float32, kind="ExternalOutput").ap())
    retention_moe_kernel(nc, *args)
    r = run_bass_kernel_spmd(nc, [{f"in_{n}": a for n, a in arrays.items()}], core_ids=[0])
    return r.results[0]["out_0"].reshape(B, T, D)
```
